# Optimizing a Trainium2 kernel written in Bass

```python
import numpy as np
import jax
import jax.numpy as jnp

def _softmax(x, axis=-1):
    return jax.nn.softmax(x, axis=axis)

def _gelu(x):
    return jax.nn.gelu(x, approximate=True)

def _silu(x):
    return jax.nn.silu(x)

def _sigmoid(x):
    return jax.nn.sigmoid(x)

def _layernorm(x, axis=-1, eps=1e-05):
    m = jnp.mean(x, axis=axis, keepdims=True)
    v = jnp.var(x, axis=axis, keepdims=True)
    return (x - m) / jnp.sqrt(v + eps)

def _scatter_add(tgt, idx, src, axis=0):
    return tgt.at[idx].add(src)

def _segment_sum(src, seg, n):
    return jax.ops.segment_sum(src, seg, n)
kernel_name = 'mk_macaron_d1_jaxref_r4_8f3172'

def setup_inputs(seed: int=0):
    np.random.seed(seed)
    _w = jnp.asarray

    def _L0_attn_setup():
        import jax, jax.numpy as jnp
        import numpy as np
        EMBED_DIM = 512
        NUM_HEADS = 16
        BLOCK_SIZE = 128

        def _flash_attention_v2(q, k, v, block_size, scale):
            B, H, S, D = q.shape
            nb = S // block_size
            qb = q.reshape(B, H, nb, block_size, D)
            kb = k.reshape(B, H, nb, block_size, D).transpose(2, 0, 1, 3, 4)
            vb = v.reshape(B, H, nb, block_size, D).transpose(2, 0, 1, 3, 4)
            out0 = jnp.zeros_like(qb)
            l0 = jnp.zeros((B, H, nb, block_size, 1), dtype=q.dtype)
            m0 = jnp.full((B, H, nb, block_size, 1), -jnp.inf, dtype=q.dtype)

            def step(carry, kv):
                out, l, m = carry
                k_j, v_j = kv
                s = jnp.einsum('bhnqd,bhkd->bhnqk', qb, k_j) * scale
                m_ij = jnp.max(s, axis=-1, keepdims=True)
                p = jnp.exp(s - m_ij)
                l_ij = jnp.sum(p, axis=-1, keepdims=True)
                m_new = jnp.maximum(m, m_ij)
                alpha = jnp.exp(m - m_new)
                beta = jnp.exp(m_ij - m_new)
                l_new = alpha * l + beta * l_ij
                pv = jnp.einsum('bhnqk,bhkd->bhnqd', p, v_j)
                out_new = alpha * l / l_new * out + beta * l_ij / l_new * pv
                return ((out_new, l_new, m_new), None)
            (out, _, _), _ = jax.lax.scan(step, (out0, l0, m0), (kb, vb))
            return out.reshape(B, H, S, D)
        key = jax.random.key(seed)
        k1, k2, k3 = jax.random.split(key, 3)
        B, S, E = (2, 1024, EMBED_DIM)
        x = jax.random.normal(k1, (B, S, E), dtype=jnp.float32)
        w_qkv = jax.random.normal(k2, (3 * E, E), dtype=jnp.float32) * 0.02
        w_out = jax.random.normal(k3, (E, E), dtype=jnp.float32) * 0.02
        b_out = jnp.zeros((E,), dtype=jnp.float32)
        return {'x': x, 'w_qkv': w_qkv, 'w_out': w_out, 'b_out': b_out}
    _L0_attn_in = _L0_attn_setup()

    def _L0_ffn_setup():
        import jax, jax.numpy as jnp
        import numpy as np
        from jax import lax
        TOP_K = 2
        NORM_TOPK = True
        W_SCALE = 0.02
        key = jax.random.key(seed)
        k1, k2, k3, k4 = jax.random.split(key, 4)
        B, S, D = (4, 512, 512)
        E, H = (8, 352)
        x = jax.random.normal(k1, (B, S, D), dtype=jnp.float32)
        gate_up_proj = jax.random.normal(k2, (E, 2 * H, D), dtype=jnp.float32) * W_SCALE
        down_proj = jax.random.normal(k3, (E, D, H), dtype=jnp.float32) * W_SCALE
        router_w = jax.random.normal(k4, (E, D), dtype=jnp.float32) * W_SCALE
        return {'x': x, 'gate_up_proj': gate_up_proj, 'down_proj': down_proj, 'router_w': router_w}
    _L0_ffn_in = _L0_ffn_setup()
    _d = {'L0_attn_x': _L0_attn_in['x'], 'L0_attn_w_qkv': _L0_attn_in['w_qkv'], 'L0_attn_w_out': _L0_attn_in['w_out'], 'L0_attn_b_out': _L0_attn_in['b_out'], 'L0_ffn_gate_up_proj': _L0_ffn_in['gate_up_proj'], 'L0_ffn_down_proj': _L0_ffn_in['down_proj'], 'L0_ffn_router_w': _L0_ffn_in['router_w']}
    _x0 = _d['L0_attn_x']
    _d['L0_attn_x'] = jax.random.normal(jax.random.fold_in(jax.random.key(seed), 1), (2, 1024, 512), dtype=_x0.dtype)
    del _x0
    return _d

def reference(L0_attn_x, L0_attn_w_qkv, L0_attn_w_out, L0_attn_b_out, L0_ffn_gate_up_proj, L0_ffn_down_proj, L0_ffn_router_w):

    def _L0_attn_ref(x, w_qkv, w_out, b_out):
        import jax, jax.numpy as jnp
        import numpy as np
        EMBED_DIM = 512
        NUM_HEADS = 16
        BLOCK_SIZE = 128

        def _flash_attention_v2(q, k, v, block_size, scale):
            B, H, S, D = q.shape
            nb = S // block_size
            qb = q.reshape(B, H, nb, block_size, D)
            kb = k.reshape(B, H, nb, block_size, D).transpose(2, 0, 1, 3, 4)
            vb = v.reshape(B, H, nb, block_size, D).transpose(2, 0, 1, 3, 4)
            out0 = jnp.zeros_like(qb)
            l0 = jnp.zeros((B, H, nb, block_size, 1), dtype=q.dtype)
            m0 = jnp.full((B, H, nb, block_size, 1), -jnp.inf, dtype=q.dtype)

            def step(carry, kv):
                out, l, m = carry
                k_j, v_j = kv
                s = jnp.einsum('bhnqd,bhkd->bhnqk', qb, k_j) * scale
                m_ij = jnp.max(s, axis=-1, keepdims=True)
                p = jnp.exp(s - m_ij)
                l_ij = jnp.sum(p, axis=-1, keepdims=True)
                m_new = jnp.maximum(m, m_ij)
                alpha = jnp.exp(m - m_new)
                beta = jnp.exp(m_ij - m_new)
                l_new = alpha * l + beta * l_ij
                pv = jnp.einsum('bhnqk,bhkd->bhnqd', p, v_j)
                out_new = alpha * l / l_new * out + beta * l_ij / l_new * pv
                return ((out_new, l_new, m_new), None)
            (out, _, _), _ = jax.lax.scan(step, (out0, l0, m0), (kb, vb))
            return out.reshape(B, H, S, D)
        B, S, E = x.shape
        H = NUM_HEADS
        D = E // H
        scale = 1.0 / np.sqrt(D).astype(np.float32)
        qkv = (x @ w_qkv.T).reshape(B, S, 3, H, D)
        q, k, v = jnp.moveaxis(qkv, 2, 0)
        q = q.transpose(0, 2, 1, 3)
        k = k.transpose(0, 2, 1, 3)
        v = v.transpose(0, 2, 1, 3)
        out = _flash_attention_v2(q, k, v, BLOCK_SIZE, scale)
        out = out.transpose(0, 2, 1, 3).reshape(B, S, E)
        return out @ w_out.T + b_out

    def _L0_ffn_ref(x, gate_up_proj, down_proj, router_w):
        import jax, jax.numpy as jnp
        import numpy as np
        from jax import lax
        TOP_K = 2
        NORM_TOPK = True
        W_SCALE = 0.02
        B, S, D = x.shape
        E = gate_up_proj.shape[0]
        h = x.reshape(-1, D)
        T = h.shape[0]
        logits = h @ router_w.T
        probs = jax.nn.softmax(logits.astype(jnp.float32), axis=-1)
        vals, idx = lax.top_k(probs, TOP_K)
        if NORM_TOPK:
            vals = vals / vals.sum(axis=-1, keepdims=True)
        combine = jnp.zeros((T, E), dtype=probs.dtype)
        combine = combine.at[jnp.arange(T)[:, None], idx].add(vals)

        def step(acc, per_expert):
            gup, dp, cw = per_expert
            gate, up = jnp.split(h @ gup.T, 2, axis=-1)
            y = jax.nn.silu(gate) * up @ dp.T
            return (acc + cw[:, None].astype(acc.dtype) * y, None)
        out, _ = lax.scan(step, jnp.zeros_like(h), (gate_up_proj, down_proj, combine.T))
        return out.reshape(B, S, D)
    x = L0_attn_x
    x = x + 0.5 * _L0_ffn_ref(_layernorm(x, axis=-1), L0_ffn_gate_up_proj, L0_ffn_down_proj, L0_ffn_router_w)
    x = x + _L0_attn_ref(_layernorm(x, axis=-1), L0_attn_w_qkv, L0_attn_w_out, L0_attn_b_out)
    x = x + 0.5 * _L0_ffn_ref(_layernorm(x, axis=-1), L0_ffn_gate_up_proj, L0_ffn_down_proj, L0_ffn_router_w)
    return x

_drawn_inputs = setup_inputs


def setup_inputs(seed=0):
    import zlib

    import numpy as np

    out = dict(_drawn_inputs(seed))
    spreads = {'L0_attn_b_out': (0.0, 0.1)}
    factors = {}
    for name, (base, spread) in spreads.items():
        noise = np.random.default_rng([zlib.crc32(name.encode()), seed]).standard_normal(out[name].shape)
        drawn = base * np.exp(spread * noise) if base else spread * noise
        out[name] = jnp.asarray(drawn.astype(out[name].dtype))
    for name, factor in factors.items():
        out[name] = (out[name] * factor).astype(out[name].dtype)
    return out
```

```python
from contextlib import ExitStack, contextmanager

import concourse.bass as bass
from concourse import mybir

ALU = mybir.AluOpType
ACT = mybir.ActivationFunctionType
AX = mybir.AxisListType
F32 = mybir.dt.float32
F32R = mybir.dt.float32r
P = 128
BANK = 512


class Count:

    def __init__(self, seq, per_seq, credit=0):
        self.base, self.per_seq, self.n = seq * per_seq + credit, per_seq, 0

    def next(self, k=1):
        self.n += k
        return self.base + self.n

    def now(self):
        return self.base + self.n

    def ago(self, k):
        return self.base + (self.n - k)


@contextmanager
def looped(i, times, per_turn):
    before = [(c, c.base, c.n) for c in per_turn]
    for c, k in per_turn.items():
        c.base = c.base + i * k
    yield
    for c, base, n in before:
        assert c.n - n == per_turn[c], (c.n - n, per_turn[c])
        c.base, c.n = base, n + per_turn[c] * times


def macaron_block(nc, x, w_gu, w_dn, w_router, w_qk, w_v, w_out, b_out, expert_rows, key_blocks, out):
    D = x.shape[1]
    KC = D // P
    SEQS = 2
    TOK = x.shape[0] // SEQS
    TT = TOK // P
    HALVES = TOK // BANK
    TPH = TT // HALVES
    NE = w_router.shape[2]
    PAIRS = w_dn.shape[0]
    TILES = 2 * PAIRS
    HEADS, DH = 16, 32
    HG = P // DH
    GROUPS = HEADS // HG
    STACK = 3 * DH
    SCALE = float(DH) ** -0.5
    EPS = 1e-5
    LOOP_PAIRS = (PAIRS - 3) // 2
    assert TILES * P == expert_rows.shape[1] and PAIRS == 3 + 2 * LOOP_PAIRS and HALVES == 2

    A_UNITS = HG * (TT * HALVES + HALVES)
    MOE_AUX = TT + 1 + HALVES + TILES * HALVES
    FINISH = GROUPS * HALVES * (1 + TT)
    AUX = 2 * MOE_AUX + TT + TT + GROUPS * (2 * HALVES + A_UNITS + HALVES) + FINISH
    GU = 2 * TILES * HALVES
    DN = 2 * PAIRS * TT + TT
    ST = GROUPS * HALVES * TT * 2
    STEPS = GROUPS * HALVES * TT
    STEP_LINKS = 3 * (7 + TT) + 2 * 9 + GROUPS * 2 * HALVES + HEADS * 2 + GROUPS * HALVES * 3
    assert AUX % 2 == 0 and DN % 2 == 0

    with ExitStack() as ctx:
        def sb(where, name, shape, dt=F32):
            return where.enter_context(nc.sbuf_tensor(name, shape, dt))

        def sem(name):
            return ctx.enter_context(nc.semaphore(name))

        x_sb = sb(ctx, "x_sb", [P, TT, D])
        hT_hi = sb(ctx, "hT_hi", [P, KC, TOK], F32R)
        hT_lo = sb(ctx, "hT_lo", [P, KC, TOK], F32R)
        ident = sb(ctx, "ident", [P, P])
        router_raw = sb(ctx, "router_raw", [P, KC, NE])
        router = sb(ctx, "router", [P, KC, 2 * NE], F32R)
        stats = sb(ctx, "stats", [P, TT, 6])
        moments = sb(ctx, "moments", [P, 5, TT])
        ln = sb(ctx, "ln", [P, 6, TT])
        block_rows = sb(ctx, "block_rows", [P, TT, P], F32R)
        head_rows = sb(ctx, "head_rows", [P, P], F32R)
        in_head = sb(ctx, "in_head", [P, HG, 1])
        one_col = sb(ctx, "one_col", [P, 2 * DH - 1])
        key_rows = sb(ctx, "key_rows", [P, TT])
        inv_sum = sb(ctx, "inv_sum", [P, BANK])

        with ExitStack() as moe:
            dn_raw = sb(moe, "dn_raw", [P, 2, D])
            dn_hi = sb(moe, "dn_hi", [P, 4, D], F32R)
            dn_lo = sb(moe, "dn_lo", [P, 4, D], F32R)
            silu = sb(moe, "silu", [P, 2, BANK])
            scaled = sb(moe, "scaled", [P, 2, BANK])
            acts = sb(moe, "acts", [P, 2, BANK])
            gu_raw = sb(moe, "gu_raw", [P, 2, 2 * KC * P])
            gu_hi = sb(moe, "gu_hi", [P, 2, 2 * KC * P], F32R)
            gu_lo = sb(moe, "gu_lo", [P, 2, 2 * KC * P], F32R)
            h_sb = sb(moe, "h_sb", [P, 2, D])
            sb(moe, "unused", [P, 1024])
            act_hi = sb(moe, "act_hi", [P, 4, TOK], F32R)
            act_lo = sb(moe, "act_lo", [P, 4, TOK], F32R)
            sel_all = sb(moe, "sel_all", [2 * NE, TILES, P])
            logits_lo = sb(moe, "logits_lo", [P, TT, NE])
            logits = sb(moe, "logits", [P, TT, NE])
            top = sb(moe, "top", [P, TT, 1])
            shifted = sb(moe, "shifted", [P, TT, NE])
            expd = sb(moe, "expd", [P, TT, NE])
            beats = sb(moe, "beats", [P, NE, TT, NE])
            rank = sb(moe, "rank", [P, TT, NE])
            picked = sb(moe, "picked", [P, TT, NE])
            total = sb(moe, "total", [P, TT, 1])
            inv_total = sb(moe, "inv_total", [P, TT, 1])
            combine = sb(moe, "combine", [P, TT, NE])
            combine_s = sb(moe, "combine_s", [P, TT, 2 * NE], F32R)
            combineT = sb(moe, "combineT", [2 * NE, TOK], F32R)
            sel = sb(moe, "sel", [2 * NE, 2, P], F32R)
        with ExitStack() as att:
            qst, kst = [], []
            for slot in range(2):
                qst.append(sb(att, f"qst{slot}", [P, HG, TOK], F32R))
                kst.append(sb(att, f"kst{slot}", [P, HG, TOK], F32R))
            probsT = sb(att, "probsT", [P, 2, HG, BANK])
            block_out = sb(att, "block_out", [P, TT, BANK])
            v_sb = sb(att, "v_sb", [P, TT, D])
            qkT_hi = sb(att, "qkT_hi", [P, 2, BANK], F32R)
            qkT_lo = sb(att, "qkT_lo", [P, 2, BANK], F32R)
            qk_hi = sb(att, "qk_hi", [P, 2, KC, P], F32R)
            with ExitStack() as under_lo:
                qk_raw = sb(under_lo, "qk_raw", [P, 2, KC, P])
            qk_lo = sb(att, "qk_lo", [P, 2, KC, P], F32R)
            first_out = sb(att, "first_out", [P, HALVES, BANK])
            block_max = sb(att, "block_max", [P, TT, TT])
            full_max = sb(att, "full_max", [P, TT, 1])
            below_max = sb(att, "below_max", [P, TT, TT])
            neg_max = sb(att, "neg_max", [P, TT, TT])
            neg_max_s = sb(att, "neg_max_s", [P, TT, TT, 2], F32R)
            beta = sb(att, "beta", [P, TT, HG, DH])
            betaT = sb(att, "betaT", [P, TOK])
            w_hi = sb(att, "w_hi", [P, BANK], F32R)
            w_lo = sb(att, "w_lo", [P, BANK], F32R)
            term = sb(att, "term", [P, 2, BANK])
            acc = sb(att, "acc", [P, BANK])

        gu_ps = ctx.enter_context(nc.psum_tensor("gu_ps", [P, 4, BANK], F32))
        aux_ps = ctx.enter_context(nc.psum_tensor("aux_ps", [P, 2, BANK], F32))
        dn_ps = ctx.enter_context(nc.psum_tensor("dn_ps", [P, 2, BANK], F32))

        x_in, x_out, const_in, bias_in = sem("x_in"), sem("x_out"), sem("const_in"), sem("bias_in")
        gu_in = [sem("gu_in0"), sem("gu_in1")]
        dn_in, sel_in, attn_w_in, qk_w_in = sem("dn_in"), sem("sel_in"), sem("attn_w_in"), sem("qk_w_in")
        stack_in = [sem(f"stack_in{k}") for k in range(2 * HALVES)]
        ident_zero, consts_done = sem("ident_zero"), sem("consts_done")
        bias_added, terms_added = sem("bias_added"), sem("terms_added")
        std_ready, h_ready, exp_ready = sem("std_ready"), sem("h_ready"), sem("exp_ready")
        silu_ready = sem("silu_ready")
        gu_hi_done, dn_hi_done = sem("gu_hi_done"), sem("dn_hi_done")
        attn_w_hi, qk_w_hi = sem("attn_w_hi"), sem("qk_w_hi")
        probs_ready = sem("probs_ready")
        ones_in_stack, beta_ready = sem("ones_in_stack"), sem("beta_ready")
        beta_zero = sem("beta_zero")
        out_copied = sem("out_copied")
        dve_step = sem("dve_step")
        var_ready, ln_ready, shifted_ready = sem("var_ready"), sem("ln_ready"), sem("shifted_ready")
        combine_ready, router_ready = sem("combine_ready"), sem("router_ready")
        aux_drained = sem("aux_drained")
        acts_done = sem("acts_done")
        act_hi_done, act_ready = sem("act_hi_done"), sem("act_ready")
        gu_lo_done, dn_lo_done = sem("gu_lo_done"), sem("dn_lo_done")
        attn_w_lo, qk_w_lo = sem("attn_w_lo"), sem("qk_w_lo")
        dn_drained = sem("dn_drained")
        below_ready, max_ready = sem("below_ready"), sem("max_ready")
        sums_drained = sem("sums_drained")
        w_ready, outT_ready = sem("w_ready"), sem("outT_ready")
        aux_full, gate_full, up_full, dn_full = sem("aux_full"), sem("gate_full"), sem("up_full"), sem("dn_full")
        scores_full, out_full = sem("scores_full"), sem("out_full")
        probs_used = sem("probs_used")

        x_rows = x.rearrange("(s t p) d -> s p t d", s=SEQS, p=P)
        out_rows = out.rearrange("(s t p) d -> s p t d", s=SEQS, p=P)

        A_GAP = 4

        def a_units():
            units = []
            for h in range(HG):
                for k in range(TT * HALVES):
                    if h and k == A_GAP:
                        units += [("row", h - 1, n) for n in range(HALVES)]
                    units.append(("scores", h, k // HALVES, k % HALVES))
            return units + [("row", HG - 1, n) for n in range(HALVES)]

        def attention_steps():
            steps = [[[], [], []] for _ in range(STEPS + 1)]
            for g in range(GROUPS):
                at = g * HALVES * TT
                steps[at + 1][0] += [("beta", g, n) for n in range(HALVES)]
                if g + 1 < GROUPS:
                    units = a_units()
                    places = [(st, pl) for st in range(2, HALVES * TT - 1) for pl in range(3)]
                    for k, (st, pl) in enumerate(places):
                        steps[at + st][pl] += units[len(units) * k // len(places):len(units) * (k + 1) // len(places)]
                if g + 2 < GROUPS:
                    steps[at + HALVES * TT - 1][2] += [("proj", part, n) for part in range(2) for n in range(HALVES)]
            for half in range(GROUPS * HALVES - 1):
                for j in range(TT):
                    steps[(half + 1) * TT + 1 + j][1] += ([("sum", half)] if j == 0 else []) + [("block", half, j)]
            return steps

        def last_units():
            half = GROUPS * HALVES - 1
            return [("sum", half)] + [("block", half, j) for j in range(TT)]

        def unit_numbers():
            order = [("A", 0, u) for u in a_units()]
            for st, places in enumerate(attention_steps()):
                for u in sum(places, []):
                    order.append(("A", st // (HALVES * TT) + 1, u) if u[0] in ("scores", "row") else u)
            order += last_units()
            return {u: k for k, u in enumerate(order)}

        NUMBER = unit_numbers()
        FIRST_PROJ = {}
        seen = len(a_units())
        for st, places in enumerate(attention_steps()):
            for u in sum(places, []):
                if u == ("proj", 0, 0):
                    FIRST_PROJ[st // (HALVES * TT) + 2] = seen
                seen += 1
        UNIT_DMAS = 16 * 3 * HG

        block = ctx.enter_context(nc.Block())

        @block.sync
        def _(sp):
            sp.sem_inc(x_out, 16)
            sp.dma_start(router_raw[:], w_router).then_inc(const_in, 16)
            sp.dma_start(key_rows[STACK:STACK + 2 * TT, :], key_blocks).then_inc(const_in, 16)
            with sp.Fori(0, SEQS) as seq:
                hi_c, lo_c = Count(seq, 2 * TILES), Count(seq, 2 * TILES)
                dhi_c, dlo_c = Count(seq, 2 * PAIRS), Count(seq, 2 * PAIRS)
                qhi_c, qlo_c = Count(seq, GROUPS), Count(seq, GROUPS)
                drained_c = Count(seq, AUX, 2)
                scores_c = Count(seq, ST)
                dn_c = Count(seq, DN, 2)

                def load_moe():
                    sp.dma_start(sel_all[:].rearrange("e j r -> e (j r)"), expert_rows).then_inc(sel_in, 16)
                    with sp.Fori(0, PAIRS) as i:
                        with looped(i, PAIRS, {hi_c: 2, lo_c: 2, dhi_c: 1, dlo_c: 1}):
                            for s in range(2):
                                sp.wait_ge(gu_hi_done, hi_c.next())
                                sp.wait_ge(gu_lo_done, lo_c.next())
                                sp.dma_start(gu_raw[:, s, :], w_gu[i * 2 + s]).then_inc(gu_in[s], 16)
                            sp.wait_ge(dn_hi_done, dhi_c.next())
                            sp.wait_ge(dn_lo_done, dlo_c.next())
                            sp.dma_start(dn_raw[:].rearrange("p a d -> p (a d)"), w_dn[i]).then_inc(dn_in, 16)

                sp.wait_ge(x_out, seq * 16 + 16)
                sp.dma_start(x_sb[:], x_rows[seq]).then_inc(x_in, 16)
                load_moe()

                sp.wait_ge(gu_hi_done, hi_c.now() + 2)
                sp.wait_ge(gu_lo_done, lo_c.now() + 2)
                sp.dma_start(gu_raw[:].rearrange("p a d -> p (a d)"), w_v).then_inc(attn_w_in, 16)
                drained_c.next(MOE_AUX + TT)
                for g in range(GROUPS):
                    sp.wait_ge(qk_w_hi, qhi_c.next())
                    sp.wait_ge(qk_w_lo, qlo_c.next())
                    if g == 0:
                        sp.wait_ge(aux_drained, drained_c.now())
                        sp.dma_start(first_out[:, 0, :], b_out.partition_broadcast(P)).then_inc(bias_in, 16)
                    sp.dma_start(qk_raw[:].rearrange("p a c f -> p (a c f)"), w_qk[g]).then_inc(qk_w_in, 16)
                    if g == 0:
                        drained_c.next(TT)
                        after_v = drained_c.n
                        drained_c.next(2 * 2 * HALVES)
                        after_proj = drained_c.n
                    for part in range(2):
                        for n in range(HALVES):
                            k = (part * HALVES + n + 1) + (g * 2 * HALVES if g < 2 else 0)
                            at = after_v + k if g < 2 else after_proj + FIRST_PROJ[g] + k
                            sp.wait_ge(aux_drained, drained_c.base + at)
                            cols = slice(n * BANK, (n + 1) * BANK)
                            stack, rows = (kst, (qkT_hi, qkT_lo, qkT_hi)) if part else (qst, (qkT_hi, qkT_hi, qkT_lo))
                            for r, src in enumerate(rows):
                                for h in range(HG):
                                    sp.dma_start(stack[g % 2][r * DH:(r + 1) * DH, h, cols].bitcast(F32),
                                                 src[h * DH:(h + 1) * DH, n, :].bitcast(F32)).then_inc(stack_in[part * HALVES + n], 16)
                scores_c.next(ST)
                sp.wait_ge(scores_full, scores_c.now())
                sp.dma_start(gu_raw[:].rearrange("p a d -> p (a d)"), w_out).then_inc(attn_w_in, 16)
                dn_c.next(PAIRS * TT + TT)
                sp.wait_ge(dn_drained, dn_c.now())
                load_moe()
                dn_c.next(PAIRS * TT)
                sp.wait_ge(dn_drained, dn_c.now())
                sp.dma_start(out_rows[seq], x_sb[:]).then_inc(x_out, 16)
            sp.wait_ge(x_out, 16 * (SEQS + 1))

        @block.gpsimd
        def _(pool):
            nc.gpsimd.memset(ident[:], 0.0).then_inc(ident_zero, 1)
            nc.gpsimd.memset(one_col[:], 0.0).then_inc(ident_zero, 1)
            pool.wait_ge(ident_zero, 2)
            nc.gpsimd.memset(one_col[:, DH - 1:DH], 1.0).then_inc(consts_done, 1)
            nc.gpsimd.affine_select(out=ident[:], in_=ident[:], compare_op=ALU.not_equal, fill=1.0, base=0,
                                    pattern=[[-1, P]], channel_multiplier=1).then_inc(consts_done, 1)
            with pool.Fori(0, SEQS) as seq:
                drained_c = Count(seq, AUX, 2)
                drained_c.next(MOE_AUX + TT)
                pool.wait_ge(bias_in, seq * 16 + 16)
                pool.wait_ge(aux_drained, drained_c.now())
                for t in range(TT):
                    nc.gpsimd.tensor_tensor(x_sb[:, t, :], x_sb[:, t, :], first_out[:, 0, :], ALU.add).then_inc(bias_added, 1)
                first = drained_c.next(TT + 2 * 2 * HALVES)
                for half in range(GROUPS * HALVES):
                    for j in range(1, TT):
                        pool.wait_ge(aux_drained, first + (NUMBER[("block", half, j)] + 1))
                        if half or j > 1:
                            pool.wait_ge(terms_added, seq * (GROUPS * HALVES * (TT - 1)) + (half * (TT - 1) + j - 1))
                        nc.gpsimd.tensor_tensor(acc[:], acc[:], term[:, j % 2, :], ALU.add).then_inc(terms_added, 1)

        @block.scalar
        def _(act):
            act.wait_ge(consts_done, 2)
            act.sem_inc(silu_ready, 2)
            act.sem_inc(gu_hi_done, 2)
            act.sem_inc(dn_hi_done, 1)
            act.sem_inc(qk_w_hi, 1)
            act.sem_inc(probs_ready, 2)
            act.sem_inc(out_copied, 1)
            with act.Fori(0, SEQS) as seq:
                var_c, ln_c = Count(seq, 3), Count(seq, 3)
                full_c = Count(seq, AUX)
                drained_c = Count(seq, AUX, 2)
                shifted_c = Count(seq, 2)
                gin_c = [Count(seq, 2 * PAIRS), Count(seq, 2 * PAIRS)]
                din_c = Count(seq, 2 * PAIRS)
                gate_c, up_c, freed_c = Count(seq, GU), Count(seq, GU), Count(seq, GU)
                dn_c = Count(seq, DN)
                qin_c, sel_c = Count(seq, GROUPS), Count(seq, 2)
                scores_c, used_c, out_c = Count(seq, ST), Count(seq, STEPS), Count(seq, STEPS)
                below_c = Count(seq, HEADS)

                def layer_norm():
                    act.wait_ge(var_ready, var_c.next())
                    nc.scalar.activation(ln[:, 1, :], ln[:, 0, :], ACT.Sqrt).then_inc(std_ready, 1)
                    act.wait_ge(ln_ready, ln_c.next())
                    for t in range(TT):
                        if t >= 2:
                            act.wait_ge(aux_full, full_c.next())
                        nc.scalar.activation(h_sb[:, t % 2, :], x_sb[:, t, :], ACT.Identity,
                                             scale=ln[:, 4, t:t + 1], bias=ln[:, 5, t:t + 1]).then_inc(h_ready, 1)
                    full_c.next(2)

                def split_gu(s, j):
                    act.wait_ge(gu_in[s], gin_c[s].next() * 16)
                    nc.scalar.activation(sel[:, s, :], sel_all[:, bass.ds(j, 1), :], ACT.Copy)
                    nc.scalar.activation(gu_hi[:, s, :], gu_raw[:, s, :], ACT.Copy).then_inc(gu_hi_done, 1)

                def pair(p, split_next, first=False, s0=None):
                    s0 = s0 if s0 is not None else 2 * (p % 2)
                    if not first:
                        act.wait_ge(dn_full, dn_c.now())
                    act.wait_ge(dn_in, din_c.next() * 16)
                    nc.scalar.activation(dn_hi[:, s0:s0 + 2, :], dn_raw[:], ACT.Copy).then_inc(dn_hi_done, 1)
                    for s in range(2):
                        for n in range(HALVES):
                            act.wait_ge(gate_full, gate_c.next())
                            act.wait_ge(acts_done, freed_c.next())
                            nc.scalar.activation(silu[:, n, :], gu_ps[:, n, :], ACT.Silu).then_inc(silu_ready, 1)
                        up_c.next(HALVES)
                        if split_next:
                            act.wait_ge(up_full, up_c.now())
                            split_gu(s, p * 2 + 2 + s)

                def moe():
                    act.wait_ge(sel_in, sel_c.next() * 16)
                    split_gu(0, 0)
                    split_gu(1, 1)
                    layer_norm()
                    act.wait_ge(shifted_ready, shifted_c.next())
                    nc.scalar.activation(expd[:], shifted[:], ACT.Exp).then_inc(exp_ready, 1)
                    pair(0, True, first=True)
                    pair(1, True, first=True)
                    per = {gin_c[0]: 2, gin_c[1]: 2, din_c: 2, gate_c: 4 * HALVES, up_c: 4 * HALVES,
                           freed_c: 4 * HALVES, dn_c: 2 * TT}
                    with act.Fori(0, LOOP_PAIRS) as i:
                        with looped(i, LOOP_PAIRS, per):
                            for k in range(2):
                                dn_c.next(TT)
                                pair(i * 2 + 2 + k, True, s0=2 * k)
                    dn_c.next(TT)
                    pair(PAIRS - 1, False)
                    dn_c.next(2 * TT)

                moe()
                full_c.n = MOE_AUX
                layer_norm()
                act.wait_ge(attn_w_in, seq * 32 + 16)
                nc.scalar.activation(gu_hi[:], gu_raw[:], ACT.Copy).then_inc(attn_w_hi, 1)
                drained_c.next(MOE_AUX + TT)

                def ones_for_max(slot):
                    for h in range(HG):
                        nc.scalar.activation(kst[slot][STACK:STACK + 2 * TT, h, :].rearrange("r (j k) -> r j k", k=P),
                                             key_rows[STACK:STACK + 2 * TT, :].unsqueeze(2).to_broadcast([2 * TT, TT, P]),
                                             ACT.Copy).then_inc(ones_in_stack, 1)

                def split_qk(g):
                    act.wait_ge(qk_w_in, qin_c.next() * 16)
                    nc.scalar.activation(qk_hi[:], qk_raw[:], ACT.Copy).then_inc(qk_w_hi, 1)

                split_qk(0)
                act.wait_ge(aux_drained, drained_c.now())
                ones_for_max(0)
                act.wait_ge(aux_drained, drained_c.next(TT + 2 * HALVES))
                split_qk(1)
                ones_for_max(1)
                drained_c.next(2 * HALVES)
                nc.scalar.activation(beta[:].rearrange("p t h d -> p (t h d)"), hT_hi[:].rearrange("p c t -> p (c t)")[:, 0:TT * P],
                                     ACT.Copy, scale=0.0).then_inc(beta_zero, 1)
                act.wait_ge(beta_zero, seq + 1)

                def blocks_beta(h):
                    act.wait_ge(below_ready, below_c.next())
                    nc.scalar.activation(beta[:, :, h, 0:TT], below_max[:], ACT.Exp, scale=SCALE).then_inc(beta_ready, 1)

                def copy_block(step):
                    half, j = divmod(step, TT)
                    act.wait_ge(out_full, out_c.next())
                    if half:
                        act.wait_ge(aux_drained, drained_c.base + (drained_c.n + NUMBER[("block", half - 1, j)] + 1))
                    nc.scalar.activation(block_out[:, j, :], dn_ps[:, 0, :], ACT.Copy).then_inc(out_copied, 1)

                for h in range(HG):
                    blocks_beta(h)
                for step, places in enumerate(attention_steps()):
                    if step < STEPS:
                        for pr in range(2):
                            act.wait_ge(scores_full, scores_c.next())
                            if pr == 0:
                                act.wait_ge(probs_used, used_c.next())
                            nc.scalar.activation(probsT[:, step % 2, 2 * pr:2 * pr + 2, :],
                                                 gu_ps[:, 2 * pr:2 * pr + 2, :], ACT.Exp,
                                                 scale=SCALE).then_inc(probs_ready, 1)
                    if step:
                        copy_block(step - 1)
                    for u in sum(places, []):
                        if u[0] == "row" and u[2] == 0:
                            blocks_beta(u[1])
                    g = step // (HALVES * TT)
                    if step == g * HALVES * TT and g + 2 < GROUPS:
                        act.wait_ge(aux_drained, drained_c.base + (drained_c.n + (FIRST_PROJ[g + 1] + 2 * HALVES if g else 0)))
                        split_qk(g + 2)
                act.wait_ge(attn_w_in, seq * 32 + 32)
                nc.scalar.activation(gu_hi[:], gu_raw[:], ACT.Copy).then_inc(attn_w_hi, 1)
                dn_c.next(TT)
                full_c.n = AUX - MOE_AUX
                moe()
                assert dn_c.n == DN and gate_c.n == GU and used_c.n == STEPS

        @block.vector
        def _(dve):
            v = nc.vector
            dve.sem_inc(aux_drained, 2)
            dve.sem_inc(acts_done, 2)
            dve.sem_inc(gu_lo_done, 2)
            dve.sem_inc(dn_lo_done, 1)
            dve.sem_inc(qk_w_lo, 1)
            dve.sem_inc(dn_drained, 2)
            dve.sem_inc(sums_drained, 1)
            dve.wait_ge(consts_done, 2)
            for j in range(TT):
                ins = v.tensor_copy(block_rows[:, j, :].rearrange("p (h d) -> p h d", d=DH),
                                    ident[:].rearrange("p (h d) -> p h d", d=DH)[:, :, j:j + 1].to_broadcast([P, HG, DH]))
            ins.then_inc(router_ready, 1)
            v.tensor_reduce(in_head[:], ident[:].rearrange("p (h d) -> p h d", d=DH), AX.X, ALU.add).then_inc(router_ready, 1)
            dve.wait_ge(router_ready, 2)
            v.tensor_copy(head_rows[:].rearrange("p (h d) -> p h d", d=DH),
                          in_head[:].to_broadcast([P, HG, DH])).then_inc(router_ready, 1)
            dve.wait_ge(const_in, 32)
            v.tensor_copy(router[:, :, 0:NE], router_raw[:]).then_inc(router_ready, 1)
            dve.wait_ge(router_ready, 4)
            v.tensor_tensor(router[:, :, NE:2 * NE], router_raw[:], router[:, :, 0:NE].bitcast(F32),
                            ALU.subtract).then_inc(router_ready, 1)
            with dve.Fori(0, SEQS) as seq:
                step_c = Count(seq, STEP_LINKS)
                full_c, drained_c = Count(seq, AUX), Count(seq, AUX, 2)
                std_c, exp_c = Count(seq, 3), Count(seq, 2)
                silu_c, up_c = Count(seq, GU, 2), Count(seq, GU)
                acts_c, act_hi_c = Count(seq, GU, 2), Count(seq, GU)
                ghi_c, dhi_c = Count(seq, 2 * TILES, 2), Count(seq, 2 * PAIRS, 1)
                dn_c = Count(seq, DN)
                qhi_c = Count(seq, GROUPS, 1)

                def link(ins):
                    ins.then_inc(dve_step, 1)
                    dve.wait_ge(dve_step, step_c.next())

                def aux_unit():
                    at = full_c.n % 2
                    dve.wait_ge(aux_full, full_c.next())
                    drained_c.next()
                    return aux_ps[:, at, :]

                def layer_norm():
                    for t in range(TT):
                        stat = v.bn_stats(stats[:, t, :], x_sb[:, t, :])
                    link(stat)
                    v.tensor_tensor(moments[:, 0, :], stats[:, :, 1], stats[:, :, 4], ALU.add)
                    v.tensor_tensor(moments[:, 1, :], stats[:, :, 1], stats[:, :, 4], ALU.subtract)
                    link(v.tensor_tensor(moments[:, 2, :], stats[:, :, 2], stats[:, :, 5], ALU.add))
                    v.tensor_scalar(moments[:, 3, :], moments[:, 2, :], 1.0 / D, EPS, ALU.mult, ALU.add)
                    link(v.scalar_tensor_tensor(out=moments[:, 4, :], in0=moments[:, 1, :], scalar=0.25,
                                                in1=moments[:, 1, :], op0=ALU.mult, op1=ALU.mult))
                    v.tensor_tensor(ln[:, 0, :], moments[:, 3, :], moments[:, 4, :], ALU.add).then_inc(var_ready, 1)
                    dve.wait_ge(std_ready, std_c.next())
                    link(v.reciprocal(ln[:, 2, :], ln[:, 1, :]))
                    link(v.tensor_tensor(ln[:, 3, :], ln[:, 2, :], ln[:, 2, :], ALU.mult))
                    link(v.scalar_tensor_tensor(out=ln[:, 3, :], in0=ln[:, 3, :], scalar=-0.5, in1=ln[:, 0, :],
                                                op0=ALU.mult, op1=ALU.mult))
                    link(v.scalar_tensor_tensor(out=ln[:, 4, :], in0=ln[:, 3, :], scalar=1.5, in1=ln[:, 2, :],
                                                op0=ALU.add, op1=ALU.mult))
                    v.scalar_tensor_tensor(out=ln[:, 5, :], in0=moments[:, 0, :], scalar=-0.5, in1=ln[:, 4, :],
                                           op0=ALU.mult, op1=ALU.mult).then_inc(ln_ready, 1)
                    for t in range(TT):
                        cols = slice(t * P, (t + 1) * P)
                        ps = aux_unit().rearrange("p (c q) -> p c q", c=KC)
                        link(v.tensor_copy(hT_hi[:, :, cols], ps))
                        v.tensor_tensor(hT_lo[:, :, cols], ps, hT_hi[:, :, cols].bitcast(F32),
                                        ALU.subtract).then_inc(aux_drained, 1)

                def route():
                    ps = aux_unit()[:, 0:TT * 2 * NE].rearrange("p (t e) -> p t e", t=TT)
                    link(v.tensor_copy(logits_lo[:], ps[:, :, NE:2 * NE]))
                    v.tensor_tensor(logits[:], ps[:, :, 0:NE], logits_lo[:], ALU.add).then_inc(aux_drained, 1)
                    dve.wait_ge(aux_drained, drained_c.now())
                    link(v.tensor_reduce(top[:], logits[:], AX.X, ALU.max))
                    v.tensor_tensor(shifted[:], logits[:], top[:].to_broadcast([P, TT, NE]),
                                    ALU.subtract).then_inc(shifted_ready, 1)
                    for e in range(NE):
                        for cols, op in ((slice(0, e + 1), ALU.is_gt), (slice(e + 1, NE), ALU.is_ge)):
                            k = cols.stop - cols.start
                            if k:
                                ins = v.tensor_tensor(beats[:, e, :, cols], logits[:, :, e:e + 1].to_broadcast([P, TT, k]),
                                                      logits[:, :, cols], op)
                    link(ins)
                    link(v.tensor_reduce(rank[:], beats[:].rearrange("p a t e -> p t e a"), AX.X, ALU.add))
                    dve.wait_ge(exp_ready, exp_c.next())
                    link(v.scalar_tensor_tensor(out=picked[:], in0=rank[:], scalar=2.0, in1=expd[:],
                                                op0=ALU.is_lt, op1=ALU.mult))
                    link(v.tensor_reduce(total[:], picked[:], AX.X, ALU.add))
                    link(v.reciprocal(inv_total[:], total[:]))
                    link(v.tensor_tensor(combine[:], picked[:], inv_total[:].to_broadcast([P, TT, NE]), ALU.mult))
                    link(v.tensor_copy(combine_s[:, :, 0:NE], combine[:]))
                    v.tensor_tensor(combine_s[:, :, NE:2 * NE], combine[:], combine_s[:, :, 0:NE].bitcast(F32),
                                    ALU.subtract).then_inc(combine_ready, 1)
                    for n in range(HALVES):
                        ps = aux_unit()
                        v.tensor_copy(combineT[:, n * BANK:(n + 1) * BANK], ps[0:2 * NE, :]).then_inc(aux_drained, 1)

                def split_gu(s):
                    dve.wait_ge(gu_hi_done, ghi_c.next())
                    v.tensor_tensor(gu_lo[:, s, :], gu_raw[:, s, :], gu_hi[:, s, :].bitcast(F32),
                                    ALU.subtract).then_inc(gu_lo_done, 1)

                def evacuate(s0, split_next):
                    dve.wait_ge(dn_hi_done, dhi_c.next())
                    v.tensor_tensor(dn_lo[:, s0:s0 + 2, :], dn_raw[:], dn_hi[:, s0:s0 + 2, :].bitcast(F32),
                                    ALU.subtract).then_inc(dn_lo_done, 1)
                    for s in range(2):
                        for n in range(HALVES):
                            cols = slice(n * BANK, (n + 1) * BANK)
                            dve.wait_ge(silu_ready, silu_c.next())
                            ps = aux_unit()
                            v.tensor_tensor(scaled[:, n, :], silu[:, n, :], ps, ALU.mult).then_inc(aux_drained, 1)
                            dve.wait_ge(up_full, up_c.next())
                            dve.wait_ge(aux_drained, drained_c.now())
                            v.tensor_tensor(acts[:, n, :], scaled[:, n, :], gu_ps[:, 2 + n, :],
                                            ALU.mult).then_inc(acts_done, 1)
                            dve.wait_ge(acts_done, acts_c.next())
                            v.tensor_copy(act_hi[:, s0 + s, cols], acts[:, n, :]).then_inc(act_hi_done, 1)
                            dve.wait_ge(act_hi_done, act_hi_c.next())
                            v.tensor_tensor(act_lo[:, s0 + s, cols], acts[:, n, :],
                                            act_hi[:, s0 + s, cols].bitcast(F32), ALU.subtract).then_inc(act_ready, 1)
                        if split_next:
                            split_gu(s)

                def add_down():
                    for t in range(TT):
                        at = dn_c.n % 2
                        dve.wait_ge(dn_full, dn_c.next())
                        v.scalar_tensor_tensor(out=x_sb[:, t, :], in0=dn_ps[:, at, :], scalar=0.5, in1=x_sb[:, t, :],
                                               op0=ALU.mult, op1=ALU.add).then_inc(dn_drained, 1)

                def moe():
                    layer_norm()
                    split_gu(0)
                    split_gu(1)
                    route()
                    evacuate(0, True)
                    evacuate(2, True)
                    add_down()
                    per = {full_c: 4 * HALVES, drained_c: 4 * HALVES, silu_c: 4 * HALVES, up_c: 4 * HALVES,
                           acts_c: 4 * HALVES, act_hi_c: 4 * HALVES, ghi_c: 4, dhi_c: 2, dn_c: 2 * TT}
                    with dve.Fori(0, LOOP_PAIRS) as i:
                        with looped(i, LOOP_PAIRS, per):
                            evacuate(0, True)
                            add_down()
                            evacuate(2, True)
                            add_down()
                    evacuate(0, False)
                    add_down()
                    add_down()
                    dve.wait_ge(dn_drained, dn_c.now() + 2)

                dve.wait_ge(x_in, seq * 16 + 16)
                moe()

                layer_norm()
                dve.wait_ge(attn_w_hi, seq * 2 + 1)
                v.tensor_tensor(gu_lo[:], gu_raw[:], gu_hi[:].bitcast(F32), ALU.subtract).then_inc(attn_w_lo, 1)

                def split_qk():
                    dve.wait_ge(qk_w_hi, qhi_c.next())
                    v.tensor_tensor(qk_lo[:], qk_raw[:], qk_hi[:].bitcast(F32), ALU.subtract).then_inc(qk_w_lo, 1)

                split_qk()
                for t in range(TT):
                    ps = aux_unit()
                    v.tensor_copy(v_sb[:, t, :], ps).then_inc(aux_drained, 1)

                def proj_unit(k):
                    if k >= 2:
                        g, quarter = divmod(k - 2, 2 * HALVES)
                        dve.wait_ge(stack_in[quarter], seq * (GROUPS * UNIT_DMAS) + (g + 1) * UNIT_DMAS)
                    ps = aux_unit()
                    link(v.tensor_copy(qkT_hi[:, k % 2, :], ps))
                    v.tensor_tensor(qkT_lo[:, k % 2, :], ps, qkT_hi[:, k % 2, :].bitcast(F32),
                                    ALU.subtract).then_inc(aux_drained, 1)

                def a_unit(g, u):
                    if u[0] == "scores":
                        _, h, qt, kh = u
                        ps = aux_unit().rearrange("p (j k) -> p j k", k=P)
                        v.tensor_reduce(block_max[:, qt, kh * TPH:(kh + 1) * TPH], ps, AX.X, ALU.max).then_inc(aux_drained, 1)
                        if (qt, kh) == (TT - 1, HALVES - 1):
                            dve.wait_ge(aux_drained, drained_c.now())
                            v.tensor_scalar(neg_max[:], block_max[:], -1.0, None, ALU.mult)
                            link(v.tensor_reduce(full_max[:], block_max[:], AX.X, ALU.max))
                            if g or h:
                                dve.wait_ge(beta_ready, seq * HEADS + (g * HG + h))
                            v.tensor_tensor(below_max[:], block_max[:], full_max[:].to_broadcast([P, TT, TT]),
                                            ALU.subtract).then_inc(below_ready, 1)
                            link(v.tensor_copy(neg_max_s[:, :, :, 0], neg_max[:]))
                            v.tensor_tensor(neg_max_s[:, :, :, 1], neg_max[:], neg_max_s[:, :, :, 0].bitcast(F32),
                                            ALU.subtract).then_inc(max_ready, 1)
                    else:
                        _, h, n = u
                        ps = aux_unit()
                        v.tensor_copy(qst[g % 2][STACK:STACK + 2 * TT, h, n * BANK:(n + 1) * BANK],
                                      ps[0:2 * TT, :]).then_inc(aux_drained, 1)

                def weights(half):
                    n = half % HALVES
                    dve.wait_ge(probs_used, seq * STEPS + (2 + (half + 1) * TT))
                    if half:
                        dve.wait_ge(terms_added, seq * (GROUPS * HALVES * (TT - 1)) + (half * (TT - 1) - 1))
                    v.tensor_tensor(term[:, 0, :], dn_ps[:, 1, :], betaT[:, n * BANK:(n + 1) * BANK],
                                    ALU.mult).then_inc(sums_drained, 1)
                    dve.wait_ge(sums_drained, seq * (GROUPS * HALVES) + (half + 2))
                    link(v.tensor_copy(w_hi[:], term[:, 0, :]))
                    v.tensor_tensor(w_lo[:], term[:, 0, :], w_hi[:].bitcast(F32), ALU.subtract).then_inc(w_ready, 1)

                def finish_unit(u):
                    if u[0] == "sum":
                        ps = aux_unit()
                        v.reciprocal(inv_sum[:], ps).then_inc(aux_drained, 1)
                        return
                    _, half, j = u
                    ps = aux_unit()
                    if j >= 3:
                        dve.wait_ge(terms_added, seq * (GROUPS * HALVES * (TT - 1)) + (half * (TT - 1) + j - 2))
                    if j == 0 and half > HALVES:
                        dve.wait_ge(outT_ready, seq * (GROUPS * HALVES) + half)
                    dve.wait_ge(out_copied, seq * STEPS + (half * TT + j + 2))
                    out = term[:, j % 2, :] if j else acc[:]
                    v.tensor_tensor(out, block_out[:, j, :], ps, ALU.mult).then_inc(aux_drained, 1)

                def split_out(src, half):
                    g, n = divmod(half, HALVES)
                    cols = slice(n * BANK, (n + 1) * BANK)
                    link(v.tensor_copy(hT_hi[:, g, cols], src))
                    v.tensor_tensor(hT_lo[:, g, cols], src, hT_hi[:, g, cols].bitcast(F32),
                                    ALU.subtract).then_inc(outT_ready, 1)

                def finish(half):
                    dve.wait_ge(terms_added, seq * (GROUPS * HALVES * (TT - 1)) + (half + 1) * (TT - 1))
                    if half == 0:
                        dve.wait_ge(bias_added, (seq + 1) * TT)
                    if half < HALVES:
                        link(v.tensor_tensor(first_out[:, half, :], acc[:], inv_sum[:], ALU.mult))
                        return
                    if half == HALVES:
                        for k in range(HALVES):
                            split_out(first_out[:, k, :], k)
                    link(v.tensor_tensor(acc[:], acc[:], inv_sum[:], ALU.mult))
                    split_out(acc[:], half)

                proj_units = 0
                for k in range(2 * HALVES):
                    proj_unit(k)
                split_qk()
                for k in range(2 * HALVES, 4 * HALVES):
                    proj_unit(k)
                for u in a_units():
                    a_unit(0, u)
                proj_units = 4 * HALVES
                for step, places in enumerate(attention_steps()):
                    g = step // (HALVES * TT)
                    if step == g * HALVES * TT + 1 and g + 2 < GROUPS:
                        split_qk()
                    if step % TT == 1 and step > 2 * TT:
                        finish(step // TT - 2)
                    for place in range(3):
                        for u in places[place]:
                            if u[0] in ("scores", "row"):
                                a_unit(g + 1, u)
                            elif u[0] == "proj":
                                proj_unit(proj_units)
                                proj_units += 1
                            elif u[0] == "beta":
                                v.tensor_copy(betaT[:, u[2] * BANK:(u[2] + 1) * BANK], aux_unit()).then_inc(aux_drained, 1)
                            else:
                                finish_unit(u)
                        if place == 1 and step and step % TT == 0:
                            weights(step // TT - 1)
                finish(GROUPS * HALVES - 2)
                for u in last_units():
                    finish_unit(u)
                finish(GROUPS * HALVES - 1)
                dve.wait_ge(attn_w_hi, seq * 2 + 2)
                v.tensor_tensor(gu_lo[:], gu_raw[:], gu_hi[:].bitcast(F32), ALU.subtract).then_inc(attn_w_lo, 1)
                dve.wait_ge(bias_added, (seq + 1) * TT)
                for t in range(TT):
                    at = dn_c.n % 2
                    dve.wait_ge(dn_full, dn_c.next())
                    v.tensor_tensor(x_sb[:, t, :], dn_ps[:, at, :], x_sb[:, t, :], ALU.add).then_inc(dn_drained, 1)
                dve.wait_ge(dn_drained, dn_c.now() + 2)
                moe()
                assert step_c.n == STEP_LINKS, step_c.n
                assert full_c.n == AUX and dn_c.n == DN and up_c.n == GU

        @block.tensor
        def _(pe):
            def product(ps, lhs, rhs, last=None):
                parts = [(c, a, b) for a, b in ((0, 0), (0, 1), (1, 0)) for c in range(KC)]
                for n, (c, a, b) in enumerate(parts):
                    mm = pe.matmul(ps, lhs(c, a), rhs(c, b), start=n == 0, stop=n == len(parts) - 1)
                return mm

            pe.sem_inc(probs_used, 2)
            pe.wait_ge(consts_done, 2)
            pe.wait_ge(router_ready, 5)
            with pe.Fori(0, SEQS) as seq:
                h_c = Count(seq, 3 * TT)
                aux_c = Count(seq, AUX)
                gate_c, up_c = Count(seq, GU), Count(seq, GU)
                ghi_c, glo_c = Count(seq, 2 * TILES, 2), Count(seq, 2 * TILES, 2)
                dhi_c, dlo_c = Count(seq, 2 * PAIRS, 1), Count(seq, 2 * PAIRS, 1)
                act_c = Count(seq, GU)
                dn_c = Count(seq, DN)
                cw_c = Count(seq, 2)
                qhi_c, qlo_c = Count(seq, GROUPS, 1), Count(seq, GROUPS, 1)
                max_c = Count(seq, HEADS)
                probs_c, scores_c = Count(seq, ST, 2), Count(seq, ST)

                def aux_bank():
                    at = aux_c.n % 2
                    pe.wait_ge(aux_drained, aux_c.next())
                    return aux_ps[:, at, :]

                def drained(unit):
                    pe.wait_ge(aux_drained, aux_c.base + (unit + 1 + 2))

                def hT(lo, c, cols):
                    return (hT_lo if lo else hT_hi)[:, c, cols]

                def layer_norm():
                    for t in range(TT):
                        pe.wait_ge(h_ready, h_c.next())
                        ps = aux_bank()
                        for c in range(KC):
                            mm = pe.transpose(ps[:, c * P:(c + 1) * P], h_sb[:, t % 2, c * P:(c + 1) * P], ident[:])
                        mm.then_inc(aux_full, 1)

                def unit(s, n, before_combine=None):
                    sl, cols = s % 2, slice(n * BANK, (n + 1) * BANK)

                    def w(part):
                        return lambda c, lo: (gu_lo if lo else gu_hi)[:, sl, (part * KC + c) * P:(part * KC + c + 1) * P]

                    pe.wait_ge(silu_ready, gate_c.next())
                    product(gu_ps[:, n, :], w(0), lambda c, lo: hT(lo, c, cols)).then_inc(gate_full, 1)
                    if before_combine:
                        before_combine()
                    ps = aux_bank()
                    pe.matmul(ps, sel[:, sl, :], combineT[:, cols], start=True, stop=True).then_inc(aux_full, 1)
                    pe.wait_ge(acts_done, up_c.next())
                    product(gu_ps[:, 2 + n, :], w(1), lambda c, lo: hT(lo, c, cols)).then_inc(up_full, 1)

                def gate_up(s0, before_combine=None):
                    for s in range(2):
                        pe.wait_ge(gu_hi_done, ghi_c.next())
                        pe.wait_ge(gu_lo_done, glo_c.next())
                        for n in range(HALVES):
                            unit(s, n, before_combine if (s, n) == (0, 0) else None)

                def down(s0):
                    pe.wait_ge(act_ready, act_c.next(2 * HALVES))
                    pe.wait_ge(dn_hi_done, dhi_c.next())
                    pe.wait_ge(dn_lo_done, dlo_c.next())
                    for t in range(TT):
                        cols = slice(t * P, (t + 1) * P)
                        at = dn_c.n % 2
                        pe.wait_ge(dn_drained, dn_c.next())
                        parts = [(s, a, b) for a, b in ((0, 0), (0, 1), (1, 0)) for s in (s0, s0 + 1)]
                        for n, (s, a, b) in enumerate(parts):
                            mm = pe.matmul(dn_ps[:, at, :], (act_lo if a else act_hi)[:, s, cols],
                                           (dn_lo if b else dn_hi)[:, s, :], start=n == 0, stop=n == len(parts) - 1)
                        mm.then_inc(dn_full, 1)

                def moe():
                    first = aux_c.n
                    layer_norm()
                    ps = aux_bank()
                    for t in range(TT):
                        drained(first + t)
                        cols = slice(t * P, (t + 1) * P)
                        lg = ps[:, t * 2 * NE:(t + 1) * 2 * NE]
                        for c in range(KC):
                            pe.matmul(lg, hT_hi[:, c, cols], router[:, c, :], start=c == 0, stop=False)
                        for c in range(KC):
                            mm = pe.matmul(lg[:, 0:NE], hT_lo[:, c, cols], router[:, c, 0:NE], start=False, stop=c == KC - 1)
                    mm.then_inc(aux_full, 1)
                    gate_up(0, before_combine=combine_rows)
                    gate_up(2)
                    down(0)
                    per = {aux_c: 4 * HALVES, gate_c: 4 * HALVES, up_c: 4 * HALVES, ghi_c: 4, glo_c: 4,
                           dhi_c: 2, dlo_c: 2, act_c: 4 * HALVES, dn_c: 2 * TT}
                    with pe.Fori(0, LOOP_PAIRS) as i:
                        with looped(i, LOOP_PAIRS, per):
                            gate_up(0)
                            down(2)
                            gate_up(2)
                            down(0)
                    gate_up(0)
                    down(2)
                    down(0)

                def combine_rows():
                    pe.wait_ge(combine_ready, cw_c.next())
                    for n in range(HALVES):
                        ps = aux_bank()
                        for q in range(TPH):
                            mm = pe.transpose(ps[0:2 * NE, q * P:(q + 1) * P],
                                              combine_s[:, n * TPH + q, :].bitcast(F32), ident[:])
                        mm.then_inc(aux_full, 1)
                    drained(aux_c.n - 1)

                moe()

                layer_norm()
                drained(aux_c.n - 1)
                pe.wait_ge(attn_w_hi, seq * 2 + 1)
                pe.wait_ge(attn_w_lo, seq * 2 + 1)

                def w512(c, lo):
                    w = (gu_lo if lo else gu_hi)[:].rearrange("p a (b d) -> p (a b) d", d=D)
                    return w[:, c, :]

                for t in range(TT):
                    ps = aux_bank()
                    product(ps, lambda c, lo: hT(lo, c, slice(t * P, (t + 1) * P)), w512).then_inc(aux_full, 1)

                def proj_unit(part, n):
                    if (part, n) == (0, 0):
                        pe.wait_ge(qk_w_hi, qhi_c.next())
                        pe.wait_ge(qk_w_lo, qlo_c.next())
                    ps = aux_bank()
                    product(ps, lambda c, lo: (qk_lo if lo else qk_hi)[:, part, c, :],
                            lambda c, lo: hT(lo, c, slice(n * BANK, (n + 1) * BANK))).then_inc(aux_full, 1)

                def a_unit(g, u):
                    if u[0] == "scores":
                        _, h, qt, kh = u
                        if h == qt == kh == 0:
                            for quarter in stack_in:
                                pe.wait_ge(quarter, seq * (GROUPS * UNIT_DMAS) + (g + 1) * UNIT_DMAS)
                        ps = aux_bank()
                        mm = pe.matmul(ps, qst[g % 2][0:STACK, h, qt * P:(qt + 1) * P],
                                       kst[g % 2][0:STACK, h, kh * BANK:(kh + 1) * BANK], start=True, stop=True)
                    else:
                        _, h, n = u
                        if n == 0:
                            pe.wait_ge(max_ready, max_c.next())
                        ps = aux_bank()
                        for c in range(TPH):
                            mm = pe.transpose(ps[0:2 * TT, c * P:(c + 1) * P],
                                              neg_max_s[:, n * TPH + c, :, :].rearrange("p j b -> p (j b)").bitcast(F32), ident[:])
                    mm.then_inc(aux_full, 1)

                def beta_unit(g, n):
                    if n == 0:
                        pe.wait_ge(beta_ready, seq * HEADS + (g + 1) * HG)
                    ps = aux_bank()
                    for c in range(TPH):
                        mm = pe.transpose(ps[:, c * P:(c + 1) * P],
                                          beta[:, n * TPH + c, :, :].rearrange("p h d -> p (h d)"), ident[:])
                    mm.then_inc(aux_full, 1)

                def finish_unit(u):
                    if u[0] == "sum":
                        pe.wait_ge(w_ready, seq * (GROUPS * HALVES) + (u[1] + 1))
                        lhs = head_rows[:]
                    else:
                        lhs = block_rows[:, u[2], :]
                    ps = aux_bank()
                    pe.matmul(ps, lhs, w_hi[:], start=True, stop=False)
                    pe.matmul(ps, lhs, w_lo[:], start=False, stop=True).then_inc(aux_full, 1)

                def probs_v(step):
                    half, kt = divmod(step, TT)
                    g = half // HALVES
                    probs_c.next(2)
                    pe.wait_ge(probs_ready, probs_c.now())
                    pe.wait_ge(out_copied, seq * STEPS + (step + 1))
                    for h in range(HG):
                        mm = pe.matmul(dn_ps[h * DH:(h + 1) * DH, 0, :], v_sb[:, kt, g * P + h * DH:g * P + (h + 1) * DH],
                                       probsT[:, step % 2, h, :], start=True, stop=True, tile_position=(0, h * DH))
                    mm.then_inc(out_full, 1)
                    if kt == 0:
                        pe.wait_ge(sums_drained, seq * (GROUPS * HALVES) + (half + 1))
                    for h in range(HG):
                        mm = pe.matmul(dn_ps[h * DH:(h + 1) * DH, 1, :], one_col[:, DH - 1 - kt:2 * DH - 1 - kt],
                                       probsT[:, step % 2, h, :], start=kt == 0, stop=kt == TT - 1,
                                       tile_position=(0, h * DH))
                    mm.then_inc(probs_used, 1)

                for g in range(2):
                    for part in range(2):
                        for n in range(HALVES):
                            proj_unit(part, n)
                before_units = aux_c.n
                for u in a_units():
                    a_unit(0, u)
                for step, places in enumerate(attention_steps()):
                    g, at = divmod(step, HALVES * TT)
                    n, kt = divmod(at, TT)
                    if at == 0 and g < GROUPS:
                        drained(before_units + NUMBER[("A", g, ("row", HG - 1, HALVES - 1))])
                        if g < 2:
                            pe.wait_ge(ones_in_stack, seq * 2 * HG + (g + 1) * HG)
                    for place in range(3):
                        if place < 2 and step < STEPS:
                            pe.wait_ge(probs_ready, scores_c.next())
                            for h in (2 * place, 2 * place + 1):
                                mm = pe.matmul(gu_ps[:, h, :], kst[g % 2][0:STACK + 2 * TT, h, kt * P:(kt + 1) * P],
                                               qst[g % 2][0:STACK + 2 * TT, h, n * BANK:(n + 1) * BANK], start=True, stop=True)
                            mm.then_inc(scores_full, 1)
                        if place == 2 and step:
                            probs_v(step - 1)
                        for u in places[place]:
                            if u[0] in ("scores", "row"):
                                a_unit(g + 1, u)
                            elif u[0] == "proj":
                                proj_unit(*u[1:])
                            elif u[0] == "beta":
                                beta_unit(*u[1:])
                            else:
                                finish_unit(u)
                for u in last_units():
                    finish_unit(u)
                pe.wait_ge(attn_w_hi, seq * 2 + 2)
                pe.wait_ge(attn_w_lo, seq * 2 + 2)
                pe.wait_ge(outT_ready, (seq + 1) * (GROUPS * HALVES))
                for t in range(TT):
                    at = dn_c.n % 2
                    pe.wait_ge(dn_drained, dn_c.next())
                    product(dn_ps[:, at, :], lambda c, lo: hT(lo, c, slice(t * P, (t + 1) * P)), w512).then_inc(dn_full, 1)
                moe()
                assert aux_c.n == AUX and dn_c.n == DN and up_c.n == GU

    return nc


def kernel(L0_attn_x, L0_attn_w_qkv, L0_attn_w_out, L0_attn_b_out, L0_ffn_gate_up_proj, L0_ffn_down_proj,
           L0_ffn_router_w):
    import numpy as np
    import concourse.bacc as bacc
    from concourse.bass_utils import run_bass_kernel_spmd

    def own(a):
        return np.ascontiguousarray(a)

    shape = L0_attn_x.shape
    D = shape[-1]
    KC = D // P
    E, H2, _ = L0_ffn_gate_up_proj.shape
    H = H2 // 2
    TILES = E * H // P
    gu = np.asarray(L0_ffn_gate_up_proj).reshape(E, 2, H, D).transpose(1, 0, 2, 3).reshape(2, TILES, P, KC, P)
    gu = own(gu.transpose(1, 4, 0, 3, 2)).reshape(TILES, P, 2 * KC * P)
    dn = np.asarray(L0_ffn_down_proj).transpose(0, 2, 1).reshape(TILES // 2, 2, P, D)
    dn = own(dn.transpose(0, 2, 1, 3)).reshape(TILES // 2, P, 2 * D)
    router = own(np.asarray(L0_ffn_router_w).T.reshape(KC, P, E).transpose(1, 0, 2))
    qkv = np.asarray(L0_attn_w_qkv)
    qk = own(qkv[:2 * D].reshape(2, KC, P, KC, P).transpose(1, 4, 0, 3, 2)).reshape(KC, P, 2 * KC * P)
    wv = own(qkv[2 * D:].T.reshape(KC, P, D).transpose(1, 0, 2)).reshape(P, KC * D)
    wo = own(np.asarray(L0_attn_w_out).T.reshape(KC, P, D).transpose(1, 0, 2)).reshape(P, KC * D)
    rows = np.arange(E * H) // H
    key_blocks = np.repeat(np.eye(L0_attn_x.shape[1] // P, dtype=np.float32), 2, axis=0)
    expert_rows = np.tile(np.equal(np.arange(E)[:, None], rows[None, :]), (2, 1)).astype(np.float32)

    arrays = {
        "x": own(np.asarray(L0_attn_x)).reshape(-1, D), "w_gu": gu, "w_dn": dn, "w_router": router, "w_qk": qk,
        "w_v": wv, "w_out": wo, "b_out": own(L0_attn_b_out), "expert_rows": expert_rows,
        "key_blocks": key_blocks,
    }
    nc = bacc.Bacc("TRN2", target_bir_lowering=False, num_devices=1)
    args = [nc.dram_tensor(n, a.shape, F32, kind="ExternalInput").ap() for n, a in arrays.items()]
    out = nc.dram_tensor("out", arrays["x"].shape, F32, kind="ExternalOutput").ap()
    macaron_block(nc, *args, out)
    result = run_bass_kernel_spmd(nc, [arrays], core_ids=[0])
    return result.results[0]["out"].reshape(shape)
```

```python
from contextlib import ExitStack, contextmanager

import concourse.bass as bass
from concourse import mybir

ALU = mybir.AluOpType
ACT = mybir.ActivationFunctionType
AX = mybir.AxisListType
F32 = mybir.dt.float32
F32R = mybir.dt.float32r
P = 128
BANK = 512


class Count:

    def __init__(self, seq, per_seq, credit=0):
        self.base, self.per_seq, self.n = seq * per_seq + credit, per_seq, 0

    def next(self, k=1):
        self.n += k
        return self.base + self.n

    def now(self):
        return self.base + self.n

    def ago(self, k):
        return self.base + (self.n - k)


@contextmanager
def looped(i, times, per_turn):
    before = [(c, c.base, c.n) for c in per_turn]
    for c, k in per_turn.items():
        c.base = c.base + i * k
    yield
    for c, base, n in before:
        assert c.n - n == per_turn[c], (c.n - n, per_turn[c])
        c.base, c.n = base, n + per_turn[c] * times


def macaron_block(nc, x, w_gu, w_dn, w_router, w_qk, w_v, w_out, b_out, expert_rows, key_blocks, out):
    D = x.shape[1]
    KC = D // P
    SEQS = 2
    TOK = x.shape[0] // SEQS
    TT = TOK // P
    HALVES = TOK // BANK
    TPH = TT // HALVES
    NE = w_router.shape[2]
    PAIRS = w_dn.shape[0]
    TILES = 2 * PAIRS
    HEADS, DH = 16, 32
    HG = P // DH
    GROUPS = HEADS // HG
    STACK = 3 * DH
    SCALE = float(DH) ** -0.5
    EPS = 1e-5
    LOOP_PAIRS = (PAIRS - 3) // 2
    assert TILES * P == expert_rows.shape[1] and PAIRS == 3 + 2 * LOOP_PAIRS and HALVES == 2

    A_UNITS = HG * (TT * HALVES + HALVES)
    MOE_AUX = TT + HALVES + 1 + HALVES + TILES * HALVES
    FINISH = GROUPS * HALVES * (1 + TT)
    ATT_AUX = GROUPS * (2 * HALVES + A_UNITS + HALVES) + FINISH
    AUX = 2 * MOE_AUX + TT + ATT_AUX
    GU = 2 * TILES * HALVES
    DN = 2 * PAIRS * TT + TT
    ST = GROUPS * HALVES * TT * 2
    STEPS = GROUPS * HALVES * TT
    STEP_LINKS = 3 * (7 + TT) + 2 * 9 + GROUPS * 2 * HALVES + HEADS * 2 + GROUPS * HALVES * 2 + 2
    assert AUX % 2 == 0 and DN % 2 == 0

    with ExitStack() as ctx:
        def sb(where, name, shape, dt=F32):
            return where.enter_context(nc.sbuf_tensor(name, shape, dt))

        def sem(name):
            return ctx.enter_context(nc.semaphore(name))

        x_sb = sb(ctx, "x_sb", [P, TT, D])
        hT_hi = sb(ctx, "hT_hi", [P, KC, TOK], F32R)
        hT_lo = sb(ctx, "hT_lo", [P, KC, TOK], F32R)
        ident = sb(ctx, "ident", [P, P])
        router_raw = sb(ctx, "router_raw", [P, KC, NE])
        router = sb(ctx, "router", [P, KC, 2 * NE], F32R)
        stats = sb(ctx, "stats", [P, TT, 6])
        moments = sb(ctx, "moments", [P, 5, TT])
        ln = sb(ctx, "ln", [P, 6, TT])
        block_rows = sb(ctx, "block_rows", [P, TT, P], F32R)
        head_rows = sb(ctx, "head_rows", [P, P], F32R)
        in_head = sb(ctx, "in_head", [P, HG, 1])
        one_col = sb(ctx, "one_col", [P, 2 * DH - 1])
        key_rows = sb(ctx, "key_rows", [P, TT])
        inv_sum = sb(ctx, "inv_sum", [P, BANK])
        table_out = sb(ctx, "table_out", [P, 1])

        with ExitStack() as moe:
            dn_raw = sb(moe, "dn_raw", [P, 2, D])
            dn_hi = sb(moe, "dn_hi", [P, 4, D], F32R)
            dn_lo = sb(moe, "dn_lo", [P, 4, D], F32R)
            silu = sb(moe, "silu", [P, 2, BANK])
            scaled = sb(moe, "scaled", [P, 2, BANK])
            acts = sb(moe, "acts", [P, 2, BANK])
            gu_raw = sb(moe, "gu_raw", [P, 2, 2 * KC * P])
            gu_hi = sb(moe, "gu_hi", [P, 2, 2 * KC * P], F32R)
            gu_lo = sb(moe, "gu_lo", [P, 2, 2 * KC * P], F32R)
            h_sb = sb(moe, "h_sb", [P, 2, D])
            sb(moe, "unused", [P, 1024])
            act_hi = sb(moe, "act_hi", [P, 4, TOK], F32R)
            act_lo = sb(moe, "act_lo", [P, 4, TOK], F32R)
            sel_all = sb(moe, "sel_all", [2 * NE, TILES, P])
            sel = sb(moe, "sel", [2 * NE, 2, P], F32R)
            logits_lo = sb(moe, "logits_lo", [P, TT, NE])
            logits = sb(moe, "logits", [P, TT, NE])
            top = sb(moe, "top", [P, TT, 1])
            shifted = sb(moe, "shifted", [P, TT, NE])
            expd = sb(moe, "expd", [P, TT, NE])
            beats = sb(moe, "beats", [P, NE, TT, NE])
            rank = sb(moe, "rank", [P, TT, NE])
            picked = sb(moe, "picked", [P, TT, NE])
            total = sb(moe, "total", [P, TT, 1])
            inv_total = sb(moe, "inv_total", [P, TT, 1])
            combine = sb(moe, "combine", [P, TT, NE])
            combine_s = sb(moe, "combine_s", [P, TT, 2 * NE], F32R)
            with ExitStack() as under_combineT:
                logitsT_sb = sb(under_combineT, "logitsT_sb", [2 * NE, TOK])
            combineT = sb(moe, "combineT", [2 * NE, TOK], F32R)
            x_first = sb(moe, "x_first", [P, TT, D])
        with ExitStack() as att:
            qst, kst = [], []
            for slot in range(2):
                qst.append(sb(att, f"qst{slot}", [P, HG, TOK], F32R))
                kst.append(sb(att, f"kst{slot}", [P, HG, TOK], F32R))
            probsT = sb(att, "probsT", [P, 2, HG, BANK])
            block_out = sb(att, "block_out", [P, TT, BANK])
            v_sb = sb(att, "v_sb", [P, TT, D])
            with ExitStack() as under_qk:
                wo_hi = sb(under_qk, "wo_hi", [P, KC, D], F32R)
                with ExitStack() as under_lo:
                    wo_raw = sb(under_lo, "wo_raw", [P, KC, D])
                wo_lo = sb(under_qk, "wo_lo", [P, KC, D], F32R)
            qkT_hi = sb(att, "qkT_hi", [P, 2, BANK], F32R)
            qkT_lo = sb(att, "qkT_lo", [P, 2, BANK], F32R)
            qk_hi = sb(att, "qk_hi", [P, 2, KC, P], F32R)
            with ExitStack() as under_lo:
                qk_raw = sb(under_lo, "qk_raw", [P, 2, KC, P])
            qk_lo = sb(att, "qk_lo", [P, 2, KC, P], F32R)
            first_out = sb(att, "first_out", [P, HALVES, BANK])
            block_max = sb(att, "block_max", [P, TT, TT])
            full_max = sb(att, "full_max", [P, TT, 1])
            below_max = sb(att, "below_max", [P, TT, TT])
            neg_max = sb(att, "neg_max", [P, TT, TT])
            neg_max_s = sb(att, "neg_max_s", [P, TT, TT, 2], F32R)
            beta = sb(att, "beta", [P, TT, HG, DH])
            betaT = sb(att, "betaT", [P, TOK])
            w_hi = sb(att, "w_hi", [P, BANK], F32R)
            w_lo = sb(att, "w_lo", [P, BANK], F32R)
            term = sb(att, "term", [P, 2, BANK])
            acc = sb(att, "acc", [P, BANK])

        gu_ps = ctx.enter_context(nc.psum_tensor("gu_ps", [P, 4, BANK], F32))
        aux_ps = ctx.enter_context(nc.psum_tensor("aux_ps", [P, 2, BANK], F32))
        dn_ps = ctx.enter_context(nc.psum_tensor("dn_ps", [P, 2, BANK], F32))

        x_in = [sem(f"x_in{n}") for n in range(HALVES)]
        x_out = [sem(f"x_out{n}") for n in range(HALVES)]
        const_in, bias_in = sem("const_in"), sem("bias_in")
        gu_in = [sem("gu_in0"), sem("gu_in1")]
        dn_in, sel_in, attn_w_in, qk_w_in = sem("dn_in"), sem("sel_in"), sem("attn_w_in"), sem("qk_w_in")
        stack_in = [sem(f"stack_in{k}") for k in range(2 * HALVES)]
        head_in = [sem(f"head_in{h}") for h in range(HG)]
        ident_zero, consts_done = sem("ident_zero"), sem("consts_done")
        bias_added, terms_added = sem("bias_added"), sem("terms_added")
        mean_ready = sem("mean_ready")
        x_free = sem("x_free")
        std_ready, h_ready, exp_ready = sem("std_ready"), sem("h_ready"), sem("exp_ready")
        silu_ready = sem("silu_ready")
        gu_hi_done, dn_hi_done = sem("gu_hi_done"), sem("dn_hi_done")
        attn_w_hi, qk_w_hi = sem("attn_w_hi"), sem("qk_w_hi")
        probs_ready = sem("probs_ready")
        v_drained = sem("v_drained")
        ones_in_stack, beta_ready = sem("ones_in_stack"), sem("beta_ready")
        beta_zero = sem("beta_zero")
        out_copied = sem("out_copied")
        dve_step = sem("dve_step")
        var_ready, ln_ready, shifted_ready = sem("var_ready"), sem("ln_ready"), sem("shifted_ready")
        combine_ready, router_ready = sem("combine_ready"), sem("router_ready")
        aux_drained = sem("aux_drained")
        acts_done = sem("acts_done")
        act_hi_done, act_ready = sem("act_hi_done"), sem("act_ready")
        gu_lo_done, dn_lo_done = sem("gu_lo_done"), sem("dn_lo_done")
        attn_w_lo, qk_w_lo = sem("attn_w_lo"), sem("qk_w_lo")
        dn_drained = sem("dn_drained")
        below_ready, max_ready = sem("below_ready"), sem("max_ready")
        inv_ready = sem("inv_ready")
        sums_drained = sem("sums_drained")
        w_ready, outT_ready = sem("w_ready"), sem("outT_ready")
        aux_full, gate_full, up_full, dn_full = sem("aux_full"), sem("gate_full"), sem("up_full"), sem("dn_full")
        scores_full, out_full, v_full = sem("scores_full"), sem("out_full"), sem("v_full")
        probs_used = sem("probs_used")

        x_rows = x.rearrange("(s t p) d -> s p t d", s=SEQS, p=P)
        out_rows = out.rearrange("(s t p) d -> s p t d", s=SEQS, p=P)

        WO_STEP = (GROUPS - 1) * HALVES * TT + 1
        SPLIT_STEP = 5
        INVERT_STEP = [TT - 1, 2]
        V_AHEAD = 2
        PROJ = [(0, 0), (1, 0), (0, 1), (1, 1)]
        PROJ_STEP = {(0, 0): TT - 1, (1, 0): TT + TPH - 1, (0, 1): 2 * TT - 1, (1, 1): 2 * TT - 1}
        FIRST_STEP = 3

        def queue_bank(k):
            if MOE_AUX + TT <= k < MOE_AUX + TT + ATT_AUX:
                return gu_ps[:, 2 + k % 4, :] if k % 4 < 2 else aux_ps[:, k % 4 - 2, :]
            return aux_ps[:, k % 2, :]

        A_GAP = 4

        def a_units():
            units = []
            for h in range(HG):
                for k in range(TT * HALVES):
                    if h and k == A_GAP:
                        units += [("row", h - 1, n) for n in range(HALVES)]
                    units.append(("scores", h, k // HALVES, k % HALVES))
            return units + [("row", HG - 1, n) for n in range(HALVES)]

        def attention_steps():
            steps = [[[], [], []] for _ in range(STEPS + 1)]
            for g in range(GROUPS):
                at = g * HALVES * TT
                steps[at + 1][0] += [("beta", g, n) for n in range(HALVES)]
                if g + 1 < GROUPS:
                    units = a_units()
                    places = [(st, pl) for st in range(FIRST_STEP, HALVES * TT - 1) for pl in range(3)]
                    for k, (st, pl) in enumerate(places):
                        steps[at + st][pl] += units[len(units) * k // len(places):len(units) * (k + 1) // len(places)]
                if g + 2 < GROUPS:
                    for part, n in PROJ:
                        steps[at + PROJ_STEP[part, n]][2].append(("proj", g + 2, part, n))
            for half in range(GROUPS * HALVES - 1):
                for j in range(TT):
                    steps[(half + 1) * TT + 1 + j][0 if j else 1] += ([("sum", half)] if j == 0 else []) + [("block", half, j)]
            return steps

        def last_units():
            half = GROUPS * HALVES - 1
            return [("sum", half)] + [("block", half, j) for j in range(TT)]

        def first_units():
            units = [("v", t) for t in range(TPH)] + [("proj", 0, part, n) for part, n in PROJ]
            units += [("v", t) for t in range(TPH, TPH + V_AHEAD)]
            rest = [("v", t) for t in range(TPH + V_AHEAD, TT)] + [("proj", 1, part, n) for part, n in PROJ]
            maxima = [("A", 0, u) for u in a_units()]
            for k, u in enumerate(rest):
                units += maxima[len(maxima) * k // len(rest):len(maxima) * (k + 1) // len(rest)]
                units.append(u)
            return units

        def all_units():
            order = [u for u in first_units() if u[0] != "v"]
            for st, places in enumerate(attention_steps()):
                for u in sum(places, []):
                    order.append(("A", st // (HALVES * TT) + 1, u) if u[0] in ("scores", "row") else u)
            return order + last_units()

        NUMBER = {u: k for k, u in enumerate(all_units())}
        assert len(NUMBER) == ATT_AUX
        UNIT_DMAS = 16 * 3 * HG
        STACKED = GROUPS - 1
        HEAD_DMAS = 16 * 3 * 2

        def first_slot(part, lo, n):
            return (part * 2 + lo) * HALVES + n

        block = ctx.enter_context(nc.Block())

        @block.sync
        def _(sp):
            sp.dma_start(router_raw[:], w_router).then_inc(const_in, 16)
            sp.dma_start(key_rows[STACK:STACK + 2 * TT, :], key_blocks).then_inc(const_in, 16)

            def load_sel():
                sp.dma_start(sel_all[:].rearrange("e j r -> e (j r)"), expert_rows).then_inc(sel_in, 16)

            load_sel()
            with sp.Fori(0, SEQS) as seq:
                hi_c, lo_c = Count(seq, 2 * TILES), Count(seq, 2 * TILES)
                dhi_c, dlo_c = Count(seq, 2 * PAIRS), Count(seq, 2 * PAIRS)
                drained_c = Count(seq, AUX, 2)

                def load_moe():
                    with sp.Fori(0, PAIRS) as i:
                        with looped(i, PAIRS, {hi_c: 2, lo_c: 2, dhi_c: 1, dlo_c: 1}):
                            for s in range(2):
                                sp.wait_ge(gu_hi_done, hi_c.next())
                                sp.wait_ge(gu_lo_done, lo_c.next())
                                sp.dma_start(gu_raw[:, s, :], w_gu[i * 2 + s]).then_inc(gu_in[s], 16)
                            sp.wait_ge(dn_hi_done, dhi_c.next())
                            sp.wait_ge(dn_lo_done, dlo_c.next())
                            sp.dma_start(dn_raw[:].rearrange("p a d -> p (a d)"), w_dn[i]).then_inc(dn_in, 16)

                for n in range(HALVES):
                    tiles = slice(n * TPH, (n + 1) * TPH)
                    sp.dma_start(x_first[:, tiles, :], x_rows[seq][:, tiles, :]).then_inc(x_in[n], 16)
                load_moe()

                sp.wait_ge(gu_hi_done, hi_c.now() + 2)
                sp.wait_ge(gu_lo_done, lo_c.now() + 2)
                sp.dma_start(gu_raw[:].rearrange("p a d -> p (a d)"), w_v).then_inc(attn_w_in, 16)
                before_units = drained_c.next(MOE_AUX + TT)
                for g in range(GROUPS):
                    if g == 0:
                        sp.wait_ge(aux_drained, before_units)
                        sp.dma_start(first_out[:, 0, :], b_out.partition_broadcast(P)).then_inc(bias_in, 16)
                    else:
                        sp.wait_ge(aux_drained, before_units + (NUMBER[("proj", g - 1) + PROJ[-1]] + 1))
                    sp.dma_start(qk_raw[:].rearrange("p a c f -> p (a c f)"), w_qk[g]).then_inc(qk_w_in, 16)
                    if g == 1:
                        for h in range(HG):
                            for part in range(2):
                                for r in range(3):
                                    at = first_slot(part, r == 2 - part, 0)
                                    sp.dma_start((kst if part else qst)[0][r * DH:(r + 1) * DH, h, :].bitcast(F32),
                                                 block_out[h * DH:(h + 1) * DH, at:at + HALVES, :].rearrange("p a b -> p (a b)")
                                                 ).then_inc(head_in[h], 16)
                    for k, (part, n) in enumerate(PROJ if g else []):
                        sp.wait_ge(aux_drained, before_units + (NUMBER[("proj", g, part, n)] + 1))
                        for r in range(3):
                            src = qkT_lo if r == 2 - part else qkT_hi
                            for h in range(HG):
                                sp.dma_start((kst if part else qst)[g % 2][r * DH:(r + 1) * DH, h, n * BANK:(n + 1) * BANK].bitcast(F32),
                                             src[h * DH:(h + 1) * DH, k % 2, :].bitcast(F32)).then_inc(stack_in[k], 16)
                sp.dma_start(wo_raw[:].rearrange("p c d -> p (c d)"), w_out).then_inc(attn_w_in, 16)
                sp.wait_ge(probs_used, seq * STEPS + (2 + STEPS))
                load_sel()
                load_moe()
            for stored in x_out:
                sp.wait_ge(stored, 16 * SEQS)

        @block.gpsimd
        def _(pool):
            nc.gpsimd.memset(ident[:], 0.0).then_inc(ident_zero, 1)
            nc.gpsimd.memset(one_col[:], 0.0).then_inc(ident_zero, 1)
            pool.wait_ge(ident_zero, 2)
            nc.gpsimd.memset(one_col[:, DH - 1:DH], 1.0).then_inc(consts_done, 1)
            nc.gpsimd.affine_select(out=ident[:], in_=ident[:], compare_op=ALU.not_equal, fill=1.0, base=0,
                                    pattern=[[-1, P]], channel_multiplier=1).then_inc(consts_done, 1)
            pool.sem_inc(x_free, 1)
            with pool.Fori(0, SEQS) as seq:
                drained_c = Count(seq, AUX, 2)
                drained_c.next(MOE_AUX + TT)
                pool.wait_ge(bias_in, seq * 16 + 16)
                pool.wait_ge(aux_drained, drained_c.now())
                for t in range(TT):
                    nc.gpsimd.tensor_tensor(x_sb[:, t, :], x_sb[:, t, :], first_out[:, 0, :], ALU.add).then_inc(bias_added, 1)
                first = drained_c.now()
                for half in range(GROUPS * HALVES):
                    last = half == GROUPS * HALVES - 1
                    for j in range(1, TT):
                        pool.wait_ge(aux_drained, first + (NUMBER[("block", half, j)] + 1))
                        if half or j > 1:
                            pool.wait_ge(terms_added, seq * (GROUPS * HALVES * (TT - 1)) + (half * (TT - 1) + j - 1))
                        nc.gpsimd.tensor_tensor(acc[:], acc[:], term[:, j % 2, :], ALU.add).then_inc(terms_added, 1)
                    if not last:
                        pool.wait_ge(terms_added, seq * (GROUPS * HALVES * (TT - 1)) + (half + 1) * (TT - 1))
                        pool.wait_ge(inv_ready, seq * (GROUPS * HALVES - 1) + (half + 1))
                        if half == 0:
                            pool.wait_ge(bias_added, (seq + 1) * TT)
                        nc.gpsimd.tensor_tensor(first_out[:, half, :] if half < HALVES else acc[:], acc[:], inv_sum[:],
                                                ALU.mult).then_inc(mean_ready, 1)
                for n in range(HALVES):
                    pool.wait_ge(dn_drained, seq * DN + (2 + DN - (HALVES - 1 - n) * TPH))
                    tiles = slice(n * TPH, (n + 1) * TPH)
                    pool.dma_start(out_rows[seq][:, tiles, :], x_sb[:, tiles, :]).then_inc(x_out[n], 16)
                for n in range(HALVES):
                    pool.wait_ge(x_out[n], (seq + 1) * 16)
                pool.sem_inc(x_free, 1)

        @block.scalar
        def _(act):
            act.wait_ge(consts_done, 2)
            act.sem_inc(silu_ready, 2)
            act.sem_inc(gu_hi_done, 2)
            act.sem_inc(dn_hi_done, 1)
            act.sem_inc(probs_ready, 1)
            act.sem_inc(v_drained, 2)
            act.sem_inc(out_copied, 1)
            with act.Fori(0, SEQS) as seq:
                var_c, ln_c = Count(seq, 3), Count(seq, 3)
                full_c = Count(seq, AUX)
                drained_c = Count(seq, AUX, 2)
                shifted_c = Count(seq, 2)
                gin_c = [Count(seq, 2 * PAIRS), Count(seq, 2 * PAIRS)]
                din_c = Count(seq, 2 * PAIRS)
                gate_c, up_c, freed_c = Count(seq, GU), Count(seq, GU), Count(seq, GU)
                dn_c = Count(seq, DN)
                qin_c = Count(seq, GROUPS)
                scores_c, used_c, out_c = Count(seq, ST), Count(seq, STEPS), Count(seq, STEPS)
                below_c = Count(seq, HEADS)

                def load_table(function):
                    nc.scalar.activation(table_out[:], ident[:, 0:1], function)

                def layer_norm(src, router=False):
                    load_table(ACT.Sqrt)
                    act.wait_ge(var_ready, var_c.next())
                    nc.scalar.activation(ln[:, 1, :], ln[:, 0, :], ACT.Sqrt).then_inc(std_ready, 1)
                    act.wait_ge(ln_ready, ln_c.next())
                    for t in range(TT):
                        if t >= 2:
                            act.wait_ge(aux_full, full_c.next(2 if router and t - 2 == TPH else 1))
                        nc.scalar.activation(h_sb[:, t % 2, :], src[:, t, :], ACT.Identity,
                                             scale=ln[:, 4, t:t + 1], bias=ln[:, 5, t:t + 1]).then_inc(h_ready, 1)
                    full_c.next(2)

                def split_gu(s, j):
                    act.wait_ge(gu_in[s], gin_c[s].next() * 16)
                    nc.scalar.activation(sel[:, s, :], sel_all[:, bass.ds(j, 1), :], ACT.Copy)
                    nc.scalar.activation(gu_hi[:, s, :], gu_raw[:, s, :], ACT.Copy).then_inc(gu_hi_done, 1)

                def split_dn(s0):
                    act.wait_ge(dn_in, din_c.next() * 16)
                    nc.scalar.activation(dn_hi[:, s0:s0 + 2, :], dn_raw[:], ACT.Copy).then_inc(dn_hi_done, 1)

                def pair(p, split_next, first=False, s0=None):
                    s0 = s0 if s0 is not None else 2 * (p % 2)
                    if not first:
                        act.wait_ge(dn_full, dn_c.now())
                    if not (first and s0 == 0):
                        split_dn(s0)
                    for s in range(2):
                        for n in range(HALVES):
                            act.wait_ge(gate_full, gate_c.next())
                            act.wait_ge(acts_done, freed_c.next())
                            nc.scalar.activation(silu[:, n, :], gu_ps[:, n, :], ACT.Silu).then_inc(silu_ready, 1)
                        up_c.next(HALVES)
                        if split_next:
                            act.wait_ge(up_full, up_c.now())
                            if first and s0 == 0:
                                act.wait_ge(acts_done, up_c.now() + 2)
                            split_gu(s, p * 2 + 2 + s)

                def moe(src, split_v):
                    act.wait_ge(sel_in, seq * 16 + (16 if split_v else 32))
                    split_gu(0, 0)
                    split_gu(1, 1)
                    layer_norm(src, router=True)
                    split_dn(0)
                    load_table(ACT.Exp)
                    act.wait_ge(shifted_ready, shifted_c.next())
                    nc.scalar.activation(expd[:], shifted[:], ACT.Exp).then_inc(exp_ready, 1)
                    pair(0, True, first=True)
                    pair(1, True, first=True)
                    per = {gin_c[0]: 2, gin_c[1]: 2, din_c: 2, gate_c: 4 * HALVES, up_c: 4 * HALVES,
                           freed_c: 4 * HALVES, dn_c: 2 * TT}
                    with act.Fori(0, LOOP_PAIRS) as i:
                        with looped(i, LOOP_PAIRS, per):
                            for k in range(2):
                                dn_c.next(TT)
                                pair(i * 2 + 2 + k, True, s0=2 * k)
                    dn_c.next(TT)
                    pair(PAIRS - 1, False)
                    act.wait_ge(up_full, up_c.now())
                    if split_v:
                        act.wait_ge(attn_w_in, seq * 32 + 16)
                        nc.scalar.activation(gu_hi[:], gu_raw[:], ACT.Copy).then_inc(attn_w_hi, 1)
                    dn_c.next(2 * TT)

                moe(x_first, True)
                full_c.n = MOE_AUX
                layer_norm(x_sb)
                drained_c.next(MOE_AUX + TT)

                def ones_for_max(slot):
                    for h in range(HG):
                        nc.scalar.activation(kst[slot][STACK:STACK + 2 * TT, h, :].rearrange("r (j k) -> r j k", k=P),
                                             key_rows[STACK:STACK + 2 * TT, :].unsqueeze(2).to_broadcast([2 * TT, TT, P]),
                                             ACT.Copy).then_inc(ones_in_stack, 1)

                def split_qk(g):
                    act.wait_ge(qk_w_in, qin_c.next() * 16)
                    nc.scalar.activation(qk_hi[:], qk_raw[:], ACT.Copy).then_inc(qk_w_hi, 1)

                split_qk(0)
                act.wait_ge(aux_drained, drained_c.now())
                ones_for_max(0)
                nc.scalar.activation(beta[:].rearrange("p t h d -> p (t h d)"), hT_hi[:].rearrange("p c t -> p (c t)")[:, 0:TT * P],
                                     ACT.Copy, scale=0.0).then_inc(beta_zero, 1)
                act.wait_ge(beta_zero, seq + 1)

                def blocks_beta(h):
                    act.wait_ge(below_ready, below_c.next())
                    nc.scalar.activation(beta[:, :, h, 0:TT], below_max[:], ACT.Exp, scale=SCALE).then_inc(beta_ready, 1)

                def copy_block(step):
                    half, j = divmod(step, TT)
                    act.wait_ge(out_full, out_c.next())
                    if half:
                        act.wait_ge(aux_drained, drained_c.base + (drained_c.n + NUMBER[("block", half - 1, j)] + 1))
                    nc.scalar.activation(block_out[:, j, :], dn_ps[:, 0, :], ACT.Copy).then_inc(out_copied, 1)

                for u in first_units():
                    if u[0] == "v":
                        act.wait_ge(v_full, seq * TT + (u[1] + 1))
                        nc.scalar.activation(v_sb[:, u[1], :], gu_ps[:, u[1] % 2, :], ACT.Copy).then_inc(v_drained, 1)
                    if u == ("v", TT - 1):
                        ones_for_max(1)
                    if u == ("v", TPH):
                        split_qk(1)
                    if u[0] == "A" and u[2][0] == "row" and u[2][2] == 0:
                        blocks_beta(u[2][1])
                for step, places in enumerate(attention_steps()):
                    if step < STEPS:
                        for pr in range(2):
                            act.wait_ge(scores_full, scores_c.next())
                            if pr == 0:
                                act.wait_ge(probs_used, used_c.next())
                            nc.scalar.activation(probsT[:, step % 2, 2 * pr:2 * pr + 2, :],
                                                 gu_ps[:, 0:2, :], ACT.Exp, scale=SCALE).then_inc(probs_ready, 1)
                            if pr == 0 and step:
                                copy_block(step - 1)
                    else:
                        copy_block(step - 1)
                    for u in sum(places, []):
                        if u[0] == "row" and u[2] == 0:
                            blocks_beta(u[1])
                    g = step // (HALVES * TT)
                    if step == g * HALVES * TT + SPLIT_STEP and g + 2 < GROUPS:
                        split_qk(g + 2)
                    if step == WO_STEP:
                        act.wait_ge(attn_w_in, seq * 32 + 32)
                        for quarter in stack_in:
                            act.wait_ge(quarter, (seq + 1) * (STACKED * UNIT_DMAS))
                        nc.scalar.activation(wo_hi[:], wo_raw[:], ACT.Copy).then_inc(attn_w_hi, 1)
                dn_c.next(TT)
                full_c.n = AUX - MOE_AUX
                moe(x_sb, False)
                assert dn_c.n == DN and gate_c.n == GU and used_c.n == STEPS

        @block.vector
        def _(dve):
            v = nc.vector
            dve.sem_inc(aux_drained, 2)
            dve.sem_inc(acts_done, 2)
            dve.sem_inc(gu_lo_done, 2)
            dve.sem_inc(dn_lo_done, 1)
            dve.sem_inc(dn_drained, 2)
            dve.sem_inc(sums_drained, 1)
            dve.wait_ge(consts_done, 2)
            for j in range(TT):
                ins = v.tensor_copy(block_rows[:, j, :].rearrange("p (h d) -> p h d", d=DH),
                                    ident[:].rearrange("p (h d) -> p h d", d=DH)[:, :, j:j + 1].to_broadcast([P, HG, DH]))
            ins.then_inc(router_ready, 1)
            v.tensor_reduce(in_head[:], ident[:].rearrange("p (h d) -> p h d", d=DH), AX.X, ALU.add).then_inc(router_ready, 1)
            dve.wait_ge(router_ready, 2)
            v.tensor_copy(head_rows[:].rearrange("p (h d) -> p h d", d=DH),
                          in_head[:].to_broadcast([P, HG, DH])).then_inc(router_ready, 1)
            dve.wait_ge(const_in, 32)
            v.tensor_copy(router[:, :, 0:NE], router_raw[:]).then_inc(router_ready, 1)
            dve.wait_ge(router_ready, 4)
            v.tensor_tensor(router[:, :, NE:2 * NE], router_raw[:], router[:, :, 0:NE].bitcast(F32),
                            ALU.subtract).then_inc(router_ready, 1)
            with dve.Fori(0, SEQS) as seq:
                step_c = Count(seq, STEP_LINKS)
                full_c, drained_c = Count(seq, AUX), Count(seq, AUX, 2)
                std_c, exp_c = Count(seq, 3), Count(seq, 2)
                silu_c, up_c = Count(seq, GU, 2), Count(seq, GU)
                acts_c, act_hi_c = Count(seq, GU, 2), Count(seq, GU)
                ghi_c, dhi_c = Count(seq, 2 * TILES, 2), Count(seq, 2 * PAIRS, 1)
                dn_c = Count(seq, DN)
                qhi_c = Count(seq, GROUPS)

                def link(ins):
                    ins.then_inc(dve_step, 1)
                    dve.wait_ge(dve_step, step_c.next())

                def aux_unit():
                    bank = queue_bank(full_c.n)
                    dve.wait_ge(aux_full, full_c.next())
                    drained_c.next()
                    return bank

                def layer_norm(before_std=None, router=False):
                    v.tensor_tensor(moments[:, 0, :], stats[:, :, 1], stats[:, :, 4], ALU.add)
                    v.tensor_tensor(moments[:, 1, :], stats[:, :, 1], stats[:, :, 4], ALU.subtract)
                    link(v.tensor_tensor(moments[:, 2, :], stats[:, :, 2], stats[:, :, 5], ALU.add))
                    v.tensor_scalar(moments[:, 3, :], moments[:, 2, :], 1.0 / D, EPS, ALU.mult, ALU.add)
                    link(v.scalar_tensor_tensor(out=moments[:, 4, :], in0=moments[:, 1, :], scalar=0.25,
                                                in1=moments[:, 1, :], op0=ALU.mult, op1=ALU.mult))
                    v.tensor_tensor(ln[:, 0, :], moments[:, 3, :], moments[:, 4, :], ALU.add).then_inc(var_ready, 1)
                    if before_std:
                        before_std()
                    dve.wait_ge(std_ready, std_c.next())
                    link(v.reciprocal(ln[:, 2, :], ln[:, 1, :]))
                    link(v.tensor_tensor(ln[:, 3, :], ln[:, 2, :], ln[:, 2, :], ALU.mult))
                    link(v.scalar_tensor_tensor(out=ln[:, 3, :], in0=ln[:, 3, :], scalar=-0.5, in1=ln[:, 0, :],
                                                op0=ALU.mult, op1=ALU.mult))
                    link(v.scalar_tensor_tensor(out=ln[:, 4, :], in0=ln[:, 3, :], scalar=1.5, in1=ln[:, 2, :],
                                                op0=ALU.add, op1=ALU.mult))
                    v.scalar_tensor_tensor(out=ln[:, 5, :], in0=moments[:, 0, :], scalar=-0.5, in1=ln[:, 4, :],
                                           op0=ALU.mult, op1=ALU.mult).then_inc(ln_ready, 1)
                    for t in range(TT):
                        cols = slice(t * P, (t + 1) * P)
                        ps = aux_unit().rearrange("p (c q) -> p c q", c=KC)
                        link(v.tensor_copy(hT_hi[:, :, cols], ps))
                        v.tensor_tensor(hT_lo[:, :, cols], ps, hT_hi[:, :, cols].bitcast(F32),
                                        ALU.subtract).then_inc(aux_drained, 1)
                        if router and (t + 1) % TPH == 0:
                            half = slice((t // TPH) * BANK, (t // TPH + 1) * BANK)
                            v.tensor_copy(logitsT_sb[:, half], aux_unit()[0:2 * NE, :]).then_inc(aux_drained, 1)

                def route():
                    ps = aux_unit()[:, 0:TT * 2 * NE].rearrange("p (t e) -> p t e", t=TT)
                    link(v.tensor_copy(logits_lo[:], ps[:, :, NE:2 * NE]))
                    v.tensor_tensor(logits[:], ps[:, :, 0:NE], logits_lo[:], ALU.add).then_inc(aux_drained, 1)
                    dve.wait_ge(aux_drained, drained_c.now())
                    link(v.tensor_reduce(top[:], logits[:], AX.X, ALU.max))
                    v.tensor_tensor(shifted[:], logits[:], top[:].to_broadcast([P, TT, NE]),
                                    ALU.subtract).then_inc(shifted_ready, 1)
                    for e in range(NE):
                        for cols, op in ((slice(0, e + 1), ALU.is_gt), (slice(e + 1, NE), ALU.is_ge)):
                            k = cols.stop - cols.start
                            if k:
                                ins = v.tensor_tensor(beats[:, e, :, cols], logits[:, :, e:e + 1].to_broadcast([P, TT, k]),
                                                      logits[:, :, cols], op)
                    link(ins)
                    link(v.tensor_reduce(rank[:], beats[:].rearrange("p a t e -> p t e a"), AX.X, ALU.add))
                    dve.wait_ge(exp_ready, exp_c.next())
                    link(v.scalar_tensor_tensor(out=picked[:], in0=rank[:], scalar=2.0, in1=expd[:],
                                                op0=ALU.is_lt, op1=ALU.mult))
                    link(v.tensor_reduce(total[:], picked[:], AX.X, ALU.add))
                    link(v.reciprocal(inv_total[:], total[:]))
                    link(v.tensor_tensor(combine[:], picked[:], inv_total[:].to_broadcast([P, TT, NE]), ALU.mult))
                    link(v.tensor_copy(combine_s[:, :, 0:NE], combine[:]))
                    v.tensor_tensor(combine_s[:, :, NE:2 * NE], combine[:], combine_s[:, :, 0:NE].bitcast(F32),
                                    ALU.subtract).then_inc(combine_ready, 1)
                    for n in range(HALVES):
                        ps = aux_unit()
                        v.tensor_copy(combineT[:, n * BANK:(n + 1) * BANK], ps[0:2 * NE, :]).then_inc(aux_drained, 1)

                def split_gu(s):
                    dve.wait_ge(gu_hi_done, ghi_c.next())
                    v.tensor_tensor(gu_lo[:, s, :], gu_raw[:, s, :], gu_hi[:, s, :].bitcast(F32),
                                    ALU.subtract).then_inc(gu_lo_done, 1)

                def evacuate(s0, split_next):
                    dve.wait_ge(dn_hi_done, dhi_c.next())
                    v.tensor_tensor(dn_lo[:, s0:s0 + 2, :], dn_raw[:], dn_hi[:, s0:s0 + 2, :].bitcast(F32),
                                    ALU.subtract).then_inc(dn_lo_done, 1)
                    for s in range(2):
                        for n in range(HALVES):
                            cols = slice(n * BANK, (n + 1) * BANK)
                            dve.wait_ge(silu_ready, silu_c.next())
                            ps = aux_unit()
                            v.tensor_tensor(scaled[:, n, :], silu[:, n, :], ps, ALU.mult).then_inc(aux_drained, 1)
                            dve.wait_ge(up_full, up_c.next())
                            dve.wait_ge(aux_drained, drained_c.now())
                            v.tensor_tensor(acts[:, n, :], scaled[:, n, :], gu_ps[:, 2 + n, :],
                                            ALU.mult).then_inc(acts_done, 1)
                            dve.wait_ge(acts_done, acts_c.next())
                            v.tensor_copy(act_hi[:, s0 + s, cols], acts[:, n, :]).then_inc(act_hi_done, 1)
                            dve.wait_ge(act_hi_done, act_hi_c.next())
                            v.tensor_tensor(act_lo[:, s0 + s, cols], acts[:, n, :],
                                            act_hi[:, s0 + s, cols].bitcast(F32), ALU.subtract).then_inc(act_ready, 1)
                        if split_next:
                            split_gu(s)

                def tile_stats(t):
                    dve.wait_ge(dn_drained, dn_c.now() + (1 if t < TT - 1 else 2))
                    ins = v.bn_stats(stats[:, t, :], x_sb[:, t, :])
                    if t == TT - 1:
                        link(ins)

                def add_down(src=x_sb, last=False):
                    for t in range(TT):
                        at = dn_c.n % 2
                        dve.wait_ge(dn_full, dn_c.next())
                        v.scalar_tensor_tensor(out=x_sb[:, t, :], in0=dn_ps[:, at, :], scalar=0.5, in1=src[:, t, :],
                                               op0=ALU.mult, op1=ALU.add).then_inc(dn_drained, 1)
                        if last and t:
                            tile_stats(t - 1)
                    if last:
                        tile_stats(TT - 1)

                def moe(first):
                    if first:
                        layer_norm(before_std=lambda: split_gu(0), router=True)
                        split_gu(1)
                    else:
                        layer_norm(router=True)
                    route()
                    evacuate(0, True)
                    evacuate(2, True)
                    if first:
                        dve.wait_ge(x_free, seq + 1)
                    add_down(x_first if first else x_sb)
                    per = {full_c: 4 * HALVES, drained_c: 4 * HALVES, silu_c: 4 * HALVES, up_c: 4 * HALVES,
                           acts_c: 4 * HALVES, act_hi_c: 4 * HALVES, ghi_c: 4, dhi_c: 2, dn_c: 2 * TT}
                    with dve.Fori(0, LOOP_PAIRS) as i:
                        with looped(i, LOOP_PAIRS, per):
                            evacuate(0, True)
                            add_down()
                            evacuate(2, True)
                            add_down()
                    evacuate(0, False)
                    add_down()
                    if first:
                        dve.wait_ge(attn_w_hi, seq * 2 + 1)
                        v.tensor_tensor(gu_lo[:], gu_raw[:], gu_hi[:].bitcast(F32), ALU.subtract).then_inc(attn_w_lo, 1)
                    add_down(last=first)

                for t in range(TT):
                    if t % TPH == 0:
                        dve.wait_ge(x_in[t // TPH], seq * 16 + 16)
                    stat = v.bn_stats(stats[:, t, :], x_first[:, t, :])
                link(stat)
                moe(True)

                layer_norm()

                def split_qk():
                    dve.wait_ge(qk_w_hi, qhi_c.next())
                    v.tensor_tensor(qk_lo[:], qk_raw[:], qk_hi[:].bitcast(F32), ALU.subtract).then_inc(qk_w_lo, 1)

                split_qk()

                def proj_unit(g, part, n):
                    k = PROJ.index((part, n))
                    if g:
                        hi, lo = qkT_hi[:, k % 2, :], qkT_lo[:, k % 2, :]
                    else:
                        hi, lo = block_out[:, first_slot(part, 0, n), :].bitcast(F32R), block_out[:, first_slot(part, 1, n), :]
                    if g > 1 or g and k >= 2:
                        before, quarter = divmod((g - 1) * 2 * HALVES + k - 2, 2 * HALVES)
                        dve.wait_ge(stack_in[quarter], seq * (STACKED * UNIT_DMAS) + (before + 1) * UNIT_DMAS)
                    ps = aux_unit()
                    link(v.tensor_copy(hi, ps))
                    v.tensor_tensor(lo, ps, hi.bitcast(F32), ALU.subtract).then_inc(aux_drained, 1)

                def a_unit(g, u):
                    if u[0] == "scores":
                        _, h, qt, kh = u
                        ps = aux_unit().rearrange("p (j k) -> p j k", k=P)
                        v.tensor_reduce(block_max[:, qt, kh * TPH:(kh + 1) * TPH], ps, AX.X, ALU.max).then_inc(aux_drained, 1)
                        if (qt, kh) == (TT - 1, HALVES - 1):
                            dve.wait_ge(aux_drained, drained_c.now())
                            v.tensor_scalar(neg_max[:], block_max[:], -1.0, None, ALU.mult)
                            link(v.tensor_reduce(full_max[:], block_max[:], AX.X, ALU.max))
                            if g or h:
                                dve.wait_ge(beta_ready, seq * HEADS + (g * HG + h))
                            v.tensor_tensor(below_max[:], block_max[:], full_max[:].to_broadcast([P, TT, TT]),
                                            ALU.subtract).then_inc(below_ready, 1)
                            link(v.tensor_copy(neg_max_s[:, :, :, 0], neg_max[:]))
                            v.tensor_tensor(neg_max_s[:, :, :, 1], neg_max[:], neg_max_s[:, :, :, 0].bitcast(F32),
                                            ALU.subtract).then_inc(max_ready, 1)
                    else:
                        _, h, n = u
                        ps = aux_unit()
                        v.tensor_copy(qst[g % 2][STACK:STACK + 2 * TT, h, n * BANK:(n + 1) * BANK],
                                      ps[0:2 * TT, :]).then_inc(aux_drained, 1)

                def weights(half):
                    n = half % HALVES
                    dve.wait_ge(probs_used, seq * STEPS + (2 + (half + 1) * TT))
                    if half:
                        dve.wait_ge(terms_added, seq * (GROUPS * HALVES * (TT - 1)) + (half * (TT - 1) - 1))
                    v.tensor_tensor(term[:, 0, :], dn_ps[:, 1, :], betaT[:, n * BANK:(n + 1) * BANK],
                                    ALU.mult).then_inc(sums_drained, 1)
                    dve.wait_ge(sums_drained, seq * (GROUPS * HALVES) + (half + 2))
                    link(v.tensor_copy(w_hi[:], term[:, 0, :]))
                    v.tensor_tensor(w_lo[:], term[:, 0, :], w_hi[:].bitcast(F32), ALU.subtract).then_inc(w_ready, 1)

                def finish_unit(u):
                    if u[0] == "sum":
                        ps = aux_unit()
                        v.tensor_copy(inv_sum[:], ps).then_inc(aux_drained, 1)
                        return
                    _, half, j = u
                    ps = aux_unit()
                    if j >= 3:
                        dve.wait_ge(terms_added, seq * (GROUPS * HALVES * (TT - 1)) + (half * (TT - 1) + j - 2))
                    if j == 0 and half > HALVES:
                        dve.wait_ge(outT_ready, seq * (GROUPS * HALVES) + half)
                    dve.wait_ge(out_copied, seq * STEPS + (half * TT + j + 2))
                    out = term[:, j % 2, :] if j else acc[:]
                    v.tensor_tensor(out, block_out[:, j, :], ps, ALU.mult).then_inc(aux_drained, 1)

                def split_out(src, half):
                    g, n = divmod(half, HALVES)
                    cols = slice(n * BANK, (n + 1) * BANK)
                    link(v.tensor_copy(hT_hi[:, g, cols], src))
                    v.tensor_tensor(hT_lo[:, g, cols], src, hT_hi[:, g, cols].bitcast(F32),
                                    ALU.subtract).then_inc(outT_ready, 1)

                def finish(half):
                    if half < GROUPS * HALVES - 1:
                        dve.wait_ge(mean_ready, seq * (GROUPS * HALVES - 1) + (half + 1))
                    else:
                        link(v.reciprocal(inv_sum[:], inv_sum[:]))
                        dve.wait_ge(terms_added, seq * (GROUPS * HALVES * (TT - 1)) + (half + 1) * (TT - 1))
                        link(v.tensor_tensor(acc[:], acc[:], inv_sum[:], ALU.mult))
                    if half == HALVES:
                        for k in range(HALVES):
                            split_out(first_out[:, k, :], k)
                    if half >= HALVES:
                        split_out(acc[:], half)

                before_units = drained_c.now()
                for u in first_units():
                    if u[0] == "proj":
                        if u[1:] == (1,) + PROJ[0]:
                            split_qk()
                        proj_unit(*u[1:])
                    elif u[0] == "A":
                        a_unit(0, u[2])
                for step, places in enumerate(attention_steps()):
                    g = step // (HALVES * TT)
                    if step == g * HALVES * TT + SPLIT_STEP + 1 and g + 2 < GROUPS:
                        split_qk()
                    if step == WO_STEP + 1:
                        dve.wait_ge(attn_w_hi, seq * 2 + 2)
                        v.tensor_tensor(wo_lo[:], wo_raw[:], wo_hi[:].bitcast(F32), ALU.subtract).then_inc(attn_w_lo, 1)
                    if step % TT == 1 and step > 2 * TT:
                        finish(step // TT - 2)
                    half = step // TT - 1
                    if 0 <= half < GROUPS * HALVES - 1 and step % TT == INVERT_STEP[half % HALVES]:
                        dve.wait_ge(aux_drained, before_units + (NUMBER[("sum", half)] + 1))
                        v.reciprocal(inv_sum[:], inv_sum[:]).then_inc(inv_ready, 1)
                    for place in range(3):
                        for u in places[place]:
                            if u[0] in ("scores", "row"):
                                a_unit(g + 1, u)
                            elif u[0] == "proj":
                                proj_unit(*u[1:])
                            elif u[0] == "beta":
                                v.tensor_copy(betaT[:, u[2] * BANK:(u[2] + 1) * BANK], aux_unit()).then_inc(aux_drained, 1)
                            else:
                                finish_unit(u)
                        if place == 1 and step and step % TT == 0:
                            weights(step // TT - 1)
                finish(GROUPS * HALVES - 2)
                for u in last_units():
                    finish_unit(u)
                split_gu(0)
                split_gu(1)
                dve.wait_ge(aux_drained, before_units + (NUMBER[("sum", GROUPS * HALVES - 1)] + 1))
                dve.wait_ge(bias_added, (seq + 1) * TT)
                for t in range(TT):
                    if t == 2:
                        finish(GROUPS * HALVES - 1)
                    at = dn_c.n % 2
                    dve.wait_ge(dn_full, dn_c.next())
                    v.tensor_tensor(x_sb[:, t, :], dn_ps[:, at, :], x_sb[:, t, :], ALU.add).then_inc(dn_drained, 1)
                    if t:
                        tile_stats(t - 1)
                tile_stats(TT - 1)
                moe(False)
                assert step_c.n == STEP_LINKS, step_c.n
                assert full_c.n == AUX and dn_c.n == DN and up_c.n == GU

        @block.tensor
        def _(pe):
            def product(ps, lhs, rhs, last=None):
                parts = [(c, a, b) for a, b in ((0, 0), (0, 1), (1, 0)) for c in range(KC)]
                for n, (c, a, b) in enumerate(parts):
                    mm = pe.matmul(ps, lhs(c, a), rhs(c, b), start=n == 0, stop=n == len(parts) - 1)
                return mm

            pe.sem_inc(probs_used, 2)
            pe.wait_ge(consts_done, 2)
            pe.wait_ge(router_ready, 5)
            with pe.Fori(0, SEQS) as seq:
                h_c = Count(seq, 3 * TT)
                aux_c = Count(seq, AUX)
                gate_c, up_c = Count(seq, GU), Count(seq, GU)
                ghi_c, glo_c = Count(seq, 2 * TILES, 2), Count(seq, 2 * TILES, 2)
                dhi_c, dlo_c = Count(seq, 2 * PAIRS, 1), Count(seq, 2 * PAIRS, 1)
                act_c = Count(seq, GU)
                dn_c = Count(seq, DN)
                cw_c = Count(seq, 2)
                qhi_c, qlo_c = Count(seq, GROUPS), Count(seq, GROUPS)
                max_c = Count(seq, HEADS)
                probs_c, scores_c = Count(seq, ST, 1), Count(seq, ST)

                def aux_bank():
                    k = aux_c.n
                    aux_c.next()
                    pe.wait_ge(aux_drained, aux_c.ago(2) if MOE_AUX + TT <= k < MOE_AUX + TT + ATT_AUX else aux_c.now())
                    return queue_bank(k)

                def drained(unit):
                    pe.wait_ge(aux_drained, aux_c.base + (unit + 1 + 2))

                def hT(lo, c, cols):
                    return (hT_lo if lo else hT_hi)[:, c, cols]

                def transposes(tiles):
                    for t in tiles:
                        pe.wait_ge(h_ready, h_c.next())
                        ps = aux_bank()
                        for c in range(KC):
                            mm = pe.transpose(ps[:, c * P:(c + 1) * P], h_sb[:, t % 2, c * P:(c + 1) * P], ident[:])
                        mm.then_inc(aux_full, 1)

                def weights(s, part):
                    return lambda c, lo: (gu_lo if lo else gu_hi)[:, s % 2, (part * KC + c) * P:(part * KC + c + 1) * P]

                def weights_split():
                    pe.wait_ge(gu_hi_done, ghi_c.next())
                    pe.wait_ge(gu_lo_done, glo_c.next())

                def gate(s, n):
                    pe.wait_ge(silu_ready, gate_c.next())
                    product(gu_ps[:, n, :], weights(s, 0),
                            lambda c, lo: hT(lo, c, slice(n * BANK, (n + 1) * BANK))).then_inc(gate_full, 1)

                def combine_weights(s, n):
                    ps = aux_bank()
                    pe.matmul(ps, sel[:, s % 2, :], combineT[:, n * BANK:(n + 1) * BANK],
                              start=True, stop=True).then_inc(aux_full, 1)

                def up(s, n):
                    pe.wait_ge(acts_done, up_c.next())
                    product(gu_ps[:, 2 + n, :], weights(s, 1),
                            lambda c, lo: hT(lo, c, slice(n * BANK, (n + 1) * BANK))).then_inc(up_full, 1)

                def gate_up():
                    for s in range(2):
                        weights_split()
                        for n in range(HALVES):
                            gate(s, n)
                            combine_weights(s, n)
                            up(s, n)

                def down(s0):
                    pe.wait_ge(act_ready, act_c.next(2 * HALVES))
                    pe.wait_ge(dn_hi_done, dhi_c.next())
                    pe.wait_ge(dn_lo_done, dlo_c.next())
                    for t in range(TT):
                        cols = slice(t * P, (t + 1) * P)
                        at = dn_c.n % 2
                        pe.wait_ge(dn_drained, dn_c.next())
                        parts = [(s, a, b) for a, b in ((0, 0), (0, 1), (1, 0)) for s in (s0, s0 + 1)]
                        for n, (s, a, b) in enumerate(parts):
                            mm = pe.matmul(dn_ps[:, at, :], (act_lo if a else act_hi)[:, s, cols],
                                           (dn_lo if b else dn_hi)[:, s, :], start=n == 0, stop=n == len(parts) - 1)
                        mm.then_inc(dn_full, 1)

                def logitsT(n):
                    cols = slice(n * BANK, (n + 1) * BANK)
                    ps = aux_bank()
                    for c in range(KC):
                        pe.matmul(ps[0:2 * NE, :], router[:, c, :], hT_hi[:, c, cols], start=c == 0, stop=False)
                    for c in range(KC):
                        mm = pe.matmul(ps[0:NE, :], router[:, c, 0:NE], hT_lo[:, c, cols], start=False, stop=c == KC - 1)
                    mm.then_inc(aux_full, 1)

                def logits():
                    drained(aux_c.n - 1)
                    ps = aux_bank()
                    for t in range(TT):
                        mm = pe.matmul(ps[:, t * 2 * NE:(t + 1) * 2 * NE], logitsT_sb[:, t * P:(t + 1) * P],
                                       ident[0:2 * NE, 0:2 * NE], start=True, stop=True)
                    mm.then_inc(aux_full, 1)

                def first_pair():
                    transposes(range(TPH))
                    weights_split()
                    drained(aux_c.n - 1)
                    gate(0, 0)
                    logitsT(0)
                    transposes(range(TPH, TT))
                    drained(aux_c.n - 1)
                    logitsT(1)
                    up(0, 0)
                    logits()
                    gate(0, 1)
                    up(0, 1)
                    weights_split()
                    for n in range(HALVES):
                        gate(1, n)
                    combine_rows()
                    for n in range(HALVES):
                        combine_weights(0, n)
                    for n in range(HALVES):
                        combine_weights(1, n)
                        up(1, n)

                def moe():
                    first_pair()
                    gate_up()
                    down(0)
                    per = {aux_c: 4 * HALVES, gate_c: 4 * HALVES, up_c: 4 * HALVES, ghi_c: 4, glo_c: 4,
                           dhi_c: 2, dlo_c: 2, act_c: 4 * HALVES, dn_c: 2 * TT}
                    with pe.Fori(0, LOOP_PAIRS) as i:
                        with looped(i, LOOP_PAIRS, per):
                            gate_up()
                            down(2)
                            gate_up()
                            down(0)
                    gate_up()
                    down(2)
                    down(0)

                def combine_rows():
                    pe.wait_ge(combine_ready, cw_c.next())
                    for n in range(HALVES):
                        ps = aux_bank()
                        for q in range(TPH):
                            mm = pe.transpose(ps[0:2 * NE, q * P:(q + 1) * P],
                                              combine_s[:, n * TPH + q, :].bitcast(F32), ident[:])
                        mm.then_inc(aux_full, 1)
                    drained(aux_c.n - 1)

                moe()

                transposes(range(TT))
                drained(aux_c.n - 1)
                pe.wait_ge(attn_w_hi, seq * 2 + 1)
                pe.wait_ge(attn_w_lo, seq * 2 + 1)

                def w512(c, lo):
                    w = (gu_lo if lo else gu_hi)[:].rearrange("p a (b d) -> p (a b) d", d=D)
                    return w[:, c, :]

                pe.wait_ge(silu_ready, gate_c.now() + 2)

                def v_tile(t):
                    pe.wait_ge(v_drained, seq * TT + (t + 1))
                    product(gu_ps[:, t % 2, :], lambda c, lo: hT(lo, c, slice(t * P, (t + 1) * P)), w512).then_inc(v_full, 1)

                def proj_unit(g, part, n):
                    if (part, n) == PROJ[0]:
                        pe.wait_ge(qk_w_hi, qhi_c.next())
                        pe.wait_ge(qk_w_lo, qlo_c.next())
                    ps = aux_bank()
                    product(ps, lambda c, lo: (qk_lo if lo else qk_hi)[:, part, c, :],
                            lambda c, lo: hT(lo, c, slice(n * BANK, (n + 1) * BANK))).then_inc(aux_full, 1)

                def a_unit(g, u):
                    if u[0] == "scores":
                        _, h, qt, kh = u
                        if g == 0 and qt == kh == 0:
                            pe.wait_ge(head_in[h], (seq + 1) * HEAD_DMAS)
                        if g and h == qt == kh == 0:
                            for quarter in stack_in:
                                pe.wait_ge(quarter, seq * (STACKED * UNIT_DMAS) + g * UNIT_DMAS)
                        ps = aux_bank()
                        mm = pe.matmul(ps, qst[g % 2][0:STACK, h, qt * P:(qt + 1) * P],
                                       kst[g % 2][0:STACK, h, kh * BANK:(kh + 1) * BANK], start=True, stop=True)
                    else:
                        _, h, n = u
                        if n == 0:
                            pe.wait_ge(max_ready, max_c.next())
                        ps = aux_bank()
                        for c in range(TPH):
                            mm = pe.transpose(ps[0:2 * TT, c * P:(c + 1) * P],
                                              neg_max_s[:, n * TPH + c, :, :].rearrange("p j b -> p (j b)").bitcast(F32), ident[:])
                    mm.then_inc(aux_full, 1)

                def beta_unit(g, n):
                    if n == 0:
                        pe.wait_ge(beta_ready, seq * HEADS + (g + 1) * HG)
                    ps = aux_bank()
                    for c in range(TPH):
                        mm = pe.transpose(ps[:, c * P:(c + 1) * P],
                                          beta[:, n * TPH + c, :, :].rearrange("p h d -> p (h d)"), ident[:])
                    mm.then_inc(aux_full, 1)

                def finish_unit(u):
                    if u[0] == "sum":
                        pe.wait_ge(w_ready, seq * (GROUPS * HALVES) + (u[1] + 1))
                        lhs = head_rows[:]
                    else:
                        lhs = block_rows[:, u[2], :]
                    ps = aux_bank()
                    pe.matmul(ps, lhs, w_hi[:], start=True, stop=False)
                    pe.matmul(ps, lhs, w_lo[:], start=False, stop=True).then_inc(aux_full, 1)

                def probs_v(step):
                    half, kt = divmod(step, TT)
                    g = half // HALVES
                    probs_c.next(2)
                    pe.wait_ge(probs_ready, probs_c.now())
                    pe.wait_ge(out_copied, seq * STEPS + (step + 1))
                    for h in range(HG):
                        mm = pe.matmul(dn_ps[h * DH:(h + 1) * DH, 0, :], v_sb[:, kt, g * P + h * DH:g * P + (h + 1) * DH],
                                       probsT[:, step % 2, h, :], start=True, stop=True, tile_position=(0, h * DH))
                    mm.then_inc(out_full, 1)

                def roinv_sums(step):
                    half, kt = divmod(step, TT)
                    if kt == 0:
                        pe.wait_ge(sums_drained, seq * (GROUPS * HALVES) + (half + 1))
                    for h in range(HG):
                        mm = pe.matmul(dn_ps[h * DH:(h + 1) * DH, 1, :], one_col[:, DH - 1 - kt:2 * DH - 1 - kt],
                                       probsT[:, step % 2, h, :], start=kt == 0, stop=kt == TT - 1,
                                       tile_position=(0, h * DH))
                    mm.then_inc(probs_used, 1)

                before_units = aux_c.n
                for u in first_units():
                    if u[0] == "v":
                        v_tile(u[1])
                    elif u[0] == "proj":
                        proj_unit(*u[1:])
                    else:
                        a_unit(0, u[2])
                pe.wait_ge(v_drained, (seq + 1) * TT + 2)
                for step, places in enumerate(attention_steps()):
                    g, at = divmod(step, HALVES * TT)
                    n, kt = divmod(at, TT)
                    if at == 0 and g < GROUPS:
                        drained(before_units + NUMBER[("A", g, ("row", HG - 1, HALVES - 1))])
                        if g < 2:
                            pe.wait_ge(ones_in_stack, seq * 2 * HG + (g + 1) * HG)
                    for place in range(3):
                        if place < 2 and step < STEPS:
                            pe.wait_ge(probs_ready, scores_c.next())
                            for h in (2 * place, 2 * place + 1):
                                mm = pe.matmul(gu_ps[:, h % 2, :], kst[g % 2][0:STACK + 2 * TT, h, kt * P:(kt + 1) * P],
                                               qst[g % 2][0:STACK + 2 * TT, h, n * BANK:(n + 1) * BANK], start=True, stop=True)
                            mm.then_inc(scores_full, 1)
                        if place == 2 and step:
                            roinv_sums(step - 1)
                        for u in places[place]:
                            if u[0] in ("scores", "row"):
                                a_unit(g + 1, u)
                            elif u[0] == "proj":
                                proj_unit(*u[1:])
                            elif u[0] == "beta":
                                beta_unit(*u[1:])
                            else:
                                finish_unit(u)
                        if place == 0 and step:
                            probs_v(step - 1)
                for u in last_units():
                    finish_unit(u)
                pe.wait_ge(out_copied, (seq + 1) * STEPS + 1)
                pe.wait_ge(attn_w_hi, seq * 2 + 2)
                pe.wait_ge(attn_w_lo, seq * 2 + 2)
                for t in range(TT):
                    if t % TPH == 0:
                        pe.wait_ge(outT_ready, seq * (GROUPS * HALVES) + (GROUPS * HALVES - 1 + t // TPH))
                    at = dn_c.n % 2
                    pe.wait_ge(dn_drained, dn_c.next())
                    product(dn_ps[:, at, :], lambda c, lo: hT(lo, c, slice(t * P, (t + 1) * P)),
                            lambda c, lo: (wo_lo if lo else wo_hi)[:, c, :]).then_inc(dn_full, 1)
                drained(aux_c.n - 1)
                moe()
                assert aux_c.n == AUX and dn_c.n == DN and up_c.n == GU

    return nc


def kernel(L0_attn_x, L0_attn_w_qkv, L0_attn_w_out, L0_attn_b_out, L0_ffn_gate_up_proj, L0_ffn_down_proj,
           L0_ffn_router_w):
    import numpy as np
    import concourse.bacc as bacc
    from concourse.bass_utils import run_bass_kernel_spmd

    def own(a):
        return np.ascontiguousarray(a)

    shape = L0_attn_x.shape
    D = shape[-1]
    KC = D // P
    E, H2, _ = L0_ffn_gate_up_proj.shape
    H = H2 // 2
    TILES = E * H // P
    gu = np.asarray(L0_ffn_gate_up_proj).reshape(E, 2, H, D).transpose(1, 0, 2, 3).reshape(2, TILES, P, KC, P)
    gu = own(gu.transpose(1, 4, 0, 3, 2)).reshape(TILES, P, 2 * KC * P)
    dn = np.asarray(L0_ffn_down_proj).transpose(0, 2, 1).reshape(TILES // 2, 2, P, D)
    dn = own(dn.transpose(0, 2, 1, 3)).reshape(TILES // 2, P, 2 * D)
    router = own(np.asarray(L0_ffn_router_w).T.reshape(KC, P, E).transpose(1, 0, 2))
    qkv = np.asarray(L0_attn_w_qkv)
    qk = own(qkv[:2 * D].reshape(2, KC, P, KC, P).transpose(1, 4, 0, 3, 2)).reshape(KC, P, 2 * KC * P)
    wv = own(qkv[2 * D:].T.reshape(KC, P, D).transpose(1, 0, 2)).reshape(P, KC * D)
    wo = own(np.asarray(L0_attn_w_out).T.reshape(KC, P, D).transpose(1, 0, 2)).reshape(P, KC * D)
    rows = np.arange(E * H) // H
    key_blocks = np.repeat(np.eye(L0_attn_x.shape[1] // P, dtype=np.float32), 2, axis=0)
    expert_rows = np.tile(np.equal(np.arange(E)[:, None], rows[None, :]), (2, 1)).astype(np.float32)

    arrays = {
        "x": own(np.asarray(L0_attn_x)).reshape(-1, D), "w_gu": gu, "w_dn": dn, "w_router": router, "w_qk": qk,
        "w_v": wv, "w_out": wo, "b_out": own(L0_attn_b_out), "expert_rows": expert_rows,
        "key_blocks": key_blocks,
    }
    nc = bacc.Bacc("TRN2", target_bir_lowering=False, num_devices=1)
    args = [nc.dram_tensor(n, a.shape, F32, kind="ExternalInput").ap() for n, a in arrays.items()]
    out = nc.dram_tensor("out", arrays["x"].shape, F32, kind="ExternalOutput").ap()
    macaron_block(nc, *args, out)
    result = run_bass_kernel_spmd(nc, [arrays], core_ids=[0])
    return result.results[0]["out"].reshape(shape)
```

```python
from contextlib import ExitStack, contextmanager

import concourse.bass as bass
from concourse import mybir

ALU = mybir.AluOpType
ACT = mybir.ActivationFunctionType
AX = mybir.AxisListType
F32 = mybir.dt.float32
F32R = mybir.dt.float32r
P = 128
BANK = 512


class Count:

    def __init__(self, seq, per_seq, credit=0):
        self.base, self.per_seq, self.n = seq * per_seq + credit, per_seq, 0

    def next(self, k=1):
        self.n += k
        return self.base + self.n

    def now(self):
        return self.base + self.n

    def ago(self, k):
        return self.base + (self.n - k)


@contextmanager
def looped(i, times, per_turn):
    before = [(c, c.base, c.n) for c in per_turn]
    for c, k in per_turn.items():
        c.base = c.base + i * k
    yield
    for c, base, n in before:
        assert c.n - n == per_turn[c], (c.n - n, per_turn[c])
        c.base, c.n = base, n + per_turn[c] * times


def macaron_block(nc, x, w_gu, w_dn, w_router, w_qk, w_v, w_out, b_out, expert_rows, key_blocks, out):
    D = x.shape[1]
    KC = D // P
    SEQS = 2
    TOK = x.shape[0] // SEQS
    TT = TOK // P
    HALVES = TOK // BANK
    TPH = TT // HALVES
    NE = w_router.shape[2]
    PAIRS = w_dn.shape[0]
    TILES = 2 * PAIRS
    HEADS, DH = 16, 32
    HG = P // DH
    GROUPS = HEADS // HG
    STACK = 3 * DH
    SCALE = float(DH) ** -0.5
    EPS = 1e-5
    LOOP_PAIRS = (PAIRS - 3) // 2
    assert TILES * P == expert_rows.shape[1] and PAIRS == 3 + 2 * LOOP_PAIRS and HALVES == 2

    A_UNITS = HG * (TT * HALVES + HALVES)
    MOE_AUX = TT + HALVES + 1 + HALVES + TILES * HALVES
    FINISH = GROUPS * HALVES * (1 + TT)
    ATT_AUX = GROUPS * (2 * HALVES + A_UNITS + HALVES) + FINISH
    AUX = 2 * MOE_AUX + TT + ATT_AUX
    GU = 2 * TILES * HALVES
    DN = 2 * PAIRS * TT + TT
    ST = GROUPS * HALVES * TT * 2
    STEPS = GROUPS * HALVES * TT
    STEP_LINKS = 3 * 7 * HALVES + 2 * 9 + (GROUPS - 2) * 2 * HALVES + HEADS * 2 + GROUPS * HALVES * 2 + 2
    assert AUX % 2 == 0 and DN % 2 == 0

    with ExitStack() as ctx:
        def sb(where, name, shape, dt=F32):
            return where.enter_context(nc.sbuf_tensor(name, shape, dt))

        def sem(name):
            return ctx.enter_context(nc.semaphore(name))

        x_sb = sb(ctx, "x_sb", [P, TT, D])
        hT_hi = sb(ctx, "hT_hi", [P, KC, TOK], F32R)
        hT_lo = sb(ctx, "hT_lo", [P, KC, TOK], F32R)
        ident = sb(ctx, "ident", [P, P])
        router_raw = sb(ctx, "router_raw", [P, KC, NE])
        router = sb(ctx, "router", [P, KC, 2 * NE], F32R)
        stats = sb(ctx, "stats", [P, TT, 6])
        moments = sb(ctx, "moments", [P, 5, TT])
        ln = sb(ctx, "ln", [P, 6, TT])
        block_rows = sb(ctx, "block_rows", [P, TT, P], F32R)
        head_rows = sb(ctx, "head_rows", [P, P], F32R)
        in_head = sb(ctx, "in_head", [P, HG, 1])
        one_col = sb(ctx, "one_col", [P, 2 * DH - 1])
        key_rows = sb(ctx, "key_rows", [P, TT])
        inv_sum = sb(ctx, "inv_sum", [P, BANK])
        table_out = sb(ctx, "table_out", [P, 1])

        with ExitStack() as moe:
            dn_raw = sb(moe, "dn_raw", [P, 2, D])
            dn_hi = sb(moe, "dn_hi", [P, 4, D], F32R)
            dn_lo = sb(moe, "dn_lo", [P, 4, D], F32R)
            silu = sb(moe, "silu", [P, 2, BANK])
            scaled = sb(moe, "scaled", [P, 2, BANK])
            acts = sb(moe, "acts", [P, 2, BANK])
            gu_raw = sb(moe, "gu_raw", [P, 2, 2 * KC * P])
            gu_hi = sb(moe, "gu_hi", [P, 2, 2 * KC * P], F32R)
            gu_lo = sb(moe, "gu_lo", [P, 2, 2 * KC * P], F32R)
            h_sb = sb(moe, "h_sb", [P, 4, D])
            act_hi = sb(moe, "act_hi", [P, 4, TOK], F32R)
            act_lo = sb(moe, "act_lo", [P, 4, TOK], F32R)
            sel_all = sb(moe, "sel_all", [2 * NE, TILES, P])
            sel = sb(moe, "sel", [2 * NE, 2, P], F32R)
            logits_lo = sb(moe, "logits_lo", [P, TT, NE])
            logits = sb(moe, "logits", [P, TT, NE])
            top = sb(moe, "top", [P, TT, 1])
            shifted = sb(moe, "shifted", [P, TT, NE])
            expd = sb(moe, "expd", [P, TT, NE])
            beats = sb(moe, "beats", [P, NE, TT, NE])
            rank = sb(moe, "rank", [P, TT, NE])
            picked = sb(moe, "picked", [P, TT, NE])
            total = sb(moe, "total", [P, TT, 1])
            inv_total = sb(moe, "inv_total", [P, TT, 1])
            combine = sb(moe, "combine", [P, TT, NE])
            combine_s = sb(moe, "combine_s", [P, TT, 2 * NE], F32R)
            with ExitStack() as under_combineT:
                logitsT_sb = sb(under_combineT, "logitsT_sb", [2 * NE, TOK])
            combineT = sb(moe, "combineT", [2 * NE, TOK], F32R)
            x_first = sb(moe, "x_first", [P, TT, D])
        with ExitStack() as att:
            qst, kst = [], []
            for slot in range(2):
                qst.append(sb(att, f"qst{slot}", [P, HG, TOK], F32R))
                kst.append(sb(att, f"kst{slot}", [P, HG, TOK], F32R))
            probsT = sb(att, "probsT", [P, 2, HG, BANK])
            block_out = sb(att, "block_out", [P, TT, BANK])
            v_sb = sb(att, "v_sb", [P, TT, D])
            with ExitStack() as under_qk:
                wo_hi = sb(under_qk, "wo_hi", [P, KC, D], F32R)
                with ExitStack() as under_lo:
                    wo_raw = sb(under_lo, "wo_raw", [P, KC, D])
                wo_lo = sb(under_qk, "wo_lo", [P, KC, D], F32R)
            qkT_hi = sb(att, "qkT_hi", [P, 2, BANK], F32R)
            qkT_lo = sb(att, "qkT_lo", [P, 2, BANK], F32R)
            qk_hi = sb(att, "qk_hi", [P, 2, KC, P], F32R)
            with ExitStack() as under_lo:
                qk_raw = sb(under_lo, "qk_raw", [P, 2, KC, P])
            qk_lo = sb(att, "qk_lo", [P, 2, KC, P], F32R)
            first_out = sb(att, "first_out", [P, HALVES, BANK])
            block_max = sb(att, "block_max", [P, TT, TT])
            full_max = sb(att, "full_max", [P, TT, 1])
            below_max = sb(att, "below_max", [P, TT, TT])
            neg_max = sb(att, "neg_max", [P, TT, TT])
            neg_max_s = sb(att, "neg_max_s", [P, TT, TT, 2], F32R)
            beta = sb(att, "beta", [P, TT, HG, DH])
            betaT = sb(att, "betaT", [P, TOK])
            w_hi = sb(att, "w_hi", [P, BANK], F32R)
            w_lo = sb(att, "w_lo", [P, BANK], F32R)
            term = sb(att, "term", [P, 2, BANK])
            acc = sb(att, "acc", [P, BANK])

        gu_ps = ctx.enter_context(nc.psum_tensor("gu_ps", [P, 4, BANK], F32))
        aux_ps = ctx.enter_context(nc.psum_tensor("aux_ps", [P, 2, BANK], F32))
        dn_ps = ctx.enter_context(nc.psum_tensor("dn_ps", [P, 2, BANK], F32))

        x_in = [sem(f"x_in{n}") for n in range(HALVES)]
        x_out = [sem(f"x_out{n}") for n in range(HALVES)]
        const_in, bias_in = sem("const_in"), sem("bias_in")
        gu_in = [sem("gu_in0"), sem("gu_in1")]
        dn_in, sel_in, attn_w_in, qk_w_in = sem("dn_in"), sem("sel_in"), sem("attn_w_in"), sem("qk_w_in")
        stack_in = [sem(f"stack_in{k}") for k in range(2)]
        head_in = [sem(f"head_in{h}") for h in range(HG)]
        ident_zero, consts_done = sem("ident_zero"), sem("consts_done")
        bias_added, terms_added = sem("bias_added"), sem("terms_added")
        mean_ready = sem("mean_ready")
        x_free = sem("x_free")
        std_ready, h_ready, exp_ready = sem("std_ready"), sem("h_ready"), sem("exp_ready")
        silu_ready = sem("silu_ready")
        gu_hi_done, dn_hi_done = sem("gu_hi_done"), sem("dn_hi_done")
        attn_w_hi, qk_w_hi = sem("attn_w_hi"), sem("qk_w_hi")
        probs_ready = sem("probs_ready")
        v_drained = sem("v_drained")
        hi_ready = sem("hi_ready")
        ones_in_stack, beta_ready = sem("ones_in_stack"), sem("beta_ready")
        beta_zero = sem("beta_zero")
        out_copied = sem("out_copied")
        dve_step = sem("dve_step")
        var_ready, ln_ready, shifted_ready = sem("var_ready"), sem("ln_ready"), sem("shifted_ready")
        combine_ready, router_ready = sem("combine_ready"), sem("router_ready")
        aux_drained = sem("aux_drained")
        acts_done = sem("acts_done")
        act_hi_done, act_ready = sem("act_hi_done"), sem("act_ready")
        gu_lo_done, dn_lo_done = sem("gu_lo_done"), sem("dn_lo_done")
        attn_w_lo, qk_w_lo = sem("attn_w_lo"), sem("qk_w_lo")
        dn_drained = sem("dn_drained")
        below_ready, max_ready = sem("below_ready"), sem("max_ready")
        inv_ready = sem("inv_ready")
        sums_drained = sem("sums_drained")
        w_ready, outT_ready = sem("w_ready"), sem("outT_ready")
        aux_full, gate_full, up_full, dn_full = sem("aux_full"), sem("gate_full"), sem("up_full"), sem("dn_full")
        scores_full, out_full, v_full = sem("scores_full"), sem("out_full"), sem("v_full")
        probs_used = sem("probs_used")

        x_rows = x.rearrange("(s t p) d -> s p t d", s=SEQS, p=P)
        out_rows = out.rearrange("(s t p) d -> s p t d", s=SEQS, p=P)

        WO_STEP = (GROUPS - 1) * HALVES * TT + 1
        SPLIT_STEP = 5
        INVERT_AT = [[(TT - 1, 0), (TT - 1, 1), (TT - 1, 2), (TT - 1, 2)], [(2, 0), (2, 2), (3, 1), (4, 0)]]
        V_FIRST = 2
        V_AHEAD = 4
        PROJ = [(0, 0), (1, 0), (0, 1), (1, 1)]
        PROJ_STEP = {(0, 0): TT - 1, (1, 0): TT + TPH - 1, (0, 1): 2 * TT - 1, (1, 1): 2 * TT - 1}
        FIRST_STEP = 2

        LAST_GROUP = (GROUPS - 1) * HALVES * TT

        def wide_queue(k):
            return MOE_AUX + TT <= k < MOE_AUX + TT + NUMBER["beta", GROUPS - 1, 0]

        def after_norm_start(k):
            return k - max(start for start in (0, MOE_AUX, MOE_AUX + TT + ATT_AUX) if start <= k)

        def score_banks(step, pr):
            at = 2 * pr if step >= LAST_GROUP else 0
            return gu_ps[:, at:at + 2, :]

        def queue_bank(k):
            if after_norm_start(k) < 2:
                return gu_ps[:, 2 + k % 2, :]
            if wide_queue(k):
                return gu_ps[:, 2 + k % 4, :] if k % 4 < 2 else aux_ps[:, k % 4 - 2, :]
            return aux_ps[:, k % 2, :]

        A_GAP = 4

        def a_units():
            units = []
            for h in range(HG):
                for k in range(TT * HALVES):
                    if h and k == A_GAP:
                        units += [("row", h - 1, n) for n in range(HALVES)]
                    units.append(("scores", h, k // HALVES, k % HALVES))
            return units + [("row", HG - 1, n) for n in range(HALVES)]

        def attention_steps():
            steps = [[[], [], []] for _ in range(STEPS + 1)]
            for g in range(GROUPS):
                at = g * HALVES * TT
                steps[at + 1][0] += [("beta", g, n) for n in range(HALVES)]
                if g + 1 < GROUPS:
                    units, last_rows = a_units()[:-HALVES], a_units()[-HALVES:]
                    steps[at + HALVES * TT - 1][1] += last_rows
                    places = [(st, pl) for st in range(FIRST_STEP, HALVES * TT - 1) for pl in range(3)]
                    for k, (st, pl) in enumerate(places):
                        steps[at + st][pl] += units[len(units) * k // len(places):len(units) * (k + 1) // len(places)]
                if g + 2 < GROUPS:
                    for part, n in PROJ:
                        steps[at + PROJ_STEP[part, n]][2].append(("proj", g + 2, part, n))
            for half in range(GROUPS * HALVES - 1):
                for j in range(TT):
                    steps[(half + 1) * TT + max(j, 1)][1].append(("block", half, j))
                steps[(half + 1) * TT + 1][2].append(("sum", half))
            return steps

        def last_units():
            half = GROUPS * HALVES - 1
            return [("block", half, 0), ("sum", half)] + [("block", half, j) for j in range(1, TT)]

        def first_units():
            units = [("proj", 0, part, n) for part, n in PROJ] + [("v", t) for t in range(V_FIRST, V_AHEAD)]
            rest = [("v", t) for t in range(V_AHEAD, TT)] + [("proj", 1, part, n) for part, n in PROJ]
            maxima = [("A", 0, u) for u in a_units()]
            for k, u in enumerate(rest):
                units += maxima[len(maxima) * k // len(rest):len(maxima) * (k + 1) // len(rest)]
                units.append(u)
            return units[:-HALVES - 1] + units[-1:] + units[-HALVES - 1:-1]

        def all_units():
            order = [u for u in first_units() if u[0] != "v"]
            for st, places in enumerate(attention_steps()):
                for u in sum(places, []):
                    order.append(("A", st // (HALVES * TT) + 1, u) if u[0] in ("scores", "row") else u)
            return order + last_units()

        NUMBER = {u: k for k, u in enumerate(all_units())}
        assert len(NUMBER) == ATT_AUX
        UNIT_DMAS = 16 * 3 * HG
        STACKED = GROUPS - 1
        HEAD_DMAS = 16 * 3 * 2

        def first_slot(part, lo, n):
            return (part * 2 + lo) * HALVES + n

        def proj_slots(g, part, n):
            if g == 0:
                return (block_out[:, first_slot(part, 0, n), :].bitcast(F32R), block_out[:, first_slot(part, 1, n), :])
            k = PROJ.index((part, n))
            return qkT_hi[:, k % 2, :], qkT_lo[:, k % 2, :]

        def slot_free(engine, seq, g, part, n):
            k = PROJ.index((part, n))
            if g and k >= 2:
                engine.wait_ge(stack_in[k - 2], seq * (STACKED * UNIT_DMAS) + g * UNIT_DMAS)
            elif g > 1:
                for head in head_in:
                    engine.wait_ge(head, seq * (GROUPS * HEAD_DMAS) + g * HEAD_DMAS)

        block = ctx.enter_context(nc.Block())

        @block.sync
        def _(sp):
            sp.dma_start(router_raw[:], w_router).then_inc(const_in, 16)
            sp.dma_start(key_rows[STACK:STACK + 2 * TT, :], key_blocks).then_inc(const_in, 16)

            def load_sel():
                sp.dma_start(sel_all[:].rearrange("e j r -> e (j r)"), expert_rows).then_inc(sel_in, 16)

            load_sel()
            with sp.Fori(0, SEQS) as seq:
                hi_c, lo_c = Count(seq, 2 * TILES), Count(seq, 2 * TILES)
                dhi_c, dlo_c = Count(seq, 2 * PAIRS), Count(seq, 2 * PAIRS)
                drained_c = Count(seq, AUX, 2)

                def load_moe():
                    with sp.Fori(0, PAIRS) as i:
                        with looped(i, PAIRS, {hi_c: 2, lo_c: 2, dhi_c: 1, dlo_c: 1}):
                            for s in range(2):
                                sp.wait_ge(gu_hi_done, hi_c.next())
                                sp.wait_ge(gu_lo_done, lo_c.next())
                                sp.dma_start(gu_raw[:, s, :], w_gu[i * 2 + s]).then_inc(gu_in[s], 16)
                            sp.wait_ge(dn_hi_done, dhi_c.next())
                            sp.wait_ge(dn_lo_done, dlo_c.next())
                            sp.dma_start(dn_raw[:].rearrange("p a d -> p (a d)"), w_dn[i]).then_inc(dn_in, 16)

                for n in range(HALVES):
                    tiles = slice(n * TPH, (n + 1) * TPH)
                    sp.dma_start(x_first[:, tiles, :], x_rows[seq][:, tiles, :]).then_inc(x_in[n], 16)
                load_moe()

                sp.wait_ge(gu_hi_done, hi_c.now() + 2)
                sp.wait_ge(gu_lo_done, lo_c.now() + 2)
                sp.dma_start(gu_raw[:].rearrange("p a d -> p (a d)"), w_v).then_inc(attn_w_in, 16)
                before_units = drained_c.next(MOE_AUX + TT)
                for g in range(GROUPS):
                    if g == 0:
                        sp.dma_start(first_out[:, 0, :], b_out.partition_broadcast(P)).then_inc(bias_in, 16)
                    else:
                        sp.wait_ge(aux_drained, before_units + (NUMBER[("proj", g - 1) + PROJ[-1]] + 1))
                    if g != 1:
                        sp.dma_start(qk_raw[:].rearrange("p a c f -> p (a c f)"), w_qk[g]).then_inc(qk_w_in, 16)
                    else:
                        for h in range(HG):
                            if h == 1:
                                sp.dma_start(qk_raw[:].rearrange("p a c f -> p (a c f)"), w_qk[g]).then_inc(qk_w_in, 16)
                            for part in range(2):
                                for r in range(3):
                                    at = first_slot(part, r == 2 - part, 0)
                                    sp.dma_start((kst if part else qst)[0][r * DH:(r + 1) * DH, h, :].bitcast(F32),
                                                 block_out[h * DH:(h + 1) * DH, at:at + HALVES, :].rearrange("p a b -> p (a b)")
                                                 ).then_inc(head_in[h], 16)

                    def stack(k, h, r, done):
                        part, n = PROJ[k]
                        src = qkT_lo if r == 2 - part else qkT_hi
                        sp.dma_start((kst if part else qst)[g % 2][r * DH:(r + 1) * DH, h, n * BANK:(n + 1) * BANK].bitcast(F32),
                                     src[h * DH:(h + 1) * DH, k % 2, :].bitcast(F32)).then_inc(done, 16)

                    if g:
                        for k in range(2):
                            sp.wait_ge(aux_drained, before_units + (NUMBER[("proj", g) + PROJ[k]] + 1))
                            for r in range(3):
                                for h in range(HG):
                                    stack(k, h, r, stack_in[k])
                        sp.wait_ge(aux_drained, before_units + (NUMBER[("proj", g) + PROJ[3]] + 1))
                        for h in range(HG):
                            for k in (2, 3):
                                for r in range(3):
                                    stack(k, h, r, head_in[h])
                sp.dma_start(wo_raw[:].rearrange("p c d -> p (c d)"), w_out).then_inc(attn_w_in, 16)
                sp.wait_ge(probs_used, seq * STEPS + (2 + STEPS))
                load_sel()
                load_moe()
            for stored in x_out:
                sp.wait_ge(stored, 16 * SEQS)

        @block.gpsimd
        def _(pool):
            nc.gpsimd.memset(ident[:], 0.0).then_inc(ident_zero, 1)
            nc.gpsimd.memset(one_col[:], 0.0).then_inc(ident_zero, 1)
            pool.wait_ge(ident_zero, 2)
            nc.gpsimd.memset(one_col[:, DH - 1:DH], 1.0).then_inc(consts_done, 1)
            nc.gpsimd.affine_select(out=ident[:], in_=ident[:], compare_op=ALU.not_equal, fill=1.0, base=0,
                                    pattern=[[-1, P]], channel_multiplier=1).then_inc(consts_done, 1)
            pool.sem_inc(x_free, 1)
            with pool.Fori(0, SEQS) as seq:
                drained_c = Count(seq, AUX, 2)
                drained_c.next(MOE_AUX + TT)
                pool.wait_ge(bias_in, seq * 16 + 16)
                pool.wait_ge(aux_drained, drained_c.now())
                for t in range(TT):
                    nc.gpsimd.tensor_tensor(x_sb[:, t, :], x_sb[:, t, :], first_out[:, 0, :], ALU.add).then_inc(bias_added, 1)
                first = drained_c.now()
                for half in range(GROUPS * HALVES):
                    last = half == GROUPS * HALVES - 1
                    for j in range(1, TT):
                        pool.wait_ge(aux_drained, first + (NUMBER[("block", half, j)] + 1))
                        if half or j > 1:
                            pool.wait_ge(terms_added, seq * (GROUPS * HALVES * (TT - 1)) + (half * (TT - 1) + j - 1))
                        nc.gpsimd.tensor_tensor(acc[:], acc[:], term[:, j % 2, :], ALU.add).then_inc(terms_added, 1)
                    if not last:
                        pool.wait_ge(terms_added, seq * (GROUPS * HALVES * (TT - 1)) + (half + 1) * (TT - 1))
                        pool.wait_ge(inv_ready, seq * ((GROUPS * HALVES - 1) * 4) + (half + 1) * 4)
                        if half == 0:
                            pool.wait_ge(bias_added, (seq + 1) * TT)
                        nc.gpsimd.tensor_tensor(first_out[:, half, :] if half < HALVES else acc[:], acc[:], inv_sum[:],
                                                ALU.mult).then_inc(mean_ready, 1)
                for n in range(HALVES):
                    pool.wait_ge(dn_drained, seq * DN + (2 + DN - (HALVES - 1 - n) * TPH))
                    tiles = slice(n * TPH, (n + 1) * TPH)
                    pool.dma_start(out_rows[seq][:, tiles, :], x_sb[:, tiles, :]).then_inc(x_out[n], 16)
                for n in range(HALVES):
                    pool.wait_ge(x_out[n], (seq + 1) * 16)
                pool.sem_inc(x_free, 1)

        @block.scalar
        def _(act):
            act.wait_ge(consts_done, 2)
            act.sem_inc(silu_ready, 2)
            act.sem_inc(gu_hi_done, 2)
            act.sem_inc(dn_hi_done, 1)
            act.sem_inc(probs_ready, 1)
            act.sem_inc(v_drained, 2)
            act.sem_inc(out_copied, 1)
            with act.Fori(0, SEQS) as seq:
                var_c, ln_c = Count(seq, 3 * HALVES), Count(seq, 3 * HALVES)
                full_c = Count(seq, AUX)
                drained_c = Count(seq, AUX, 2)
                shifted_c = Count(seq, 2)
                gin_c = [Count(seq, 2 * PAIRS), Count(seq, 2 * PAIRS)]
                din_c = Count(seq, 2 * PAIRS)
                gate_c, up_c, freed_c = Count(seq, GU), Count(seq, GU), Count(seq, GU)
                dn_c = Count(seq, DN)
                qin_c = Count(seq, GROUPS)
                scores_c, used_c, out_c = Count(seq, ST), Count(seq, STEPS), Count(seq, STEPS)
                below_c = Count(seq, HEADS)

                def load_table(function):
                    nc.scalar.activation(table_out[:], ident[:, 0:1], function)

                def layer_norm(src, router=False, after_std=None):
                    def std(n):
                        half = slice(n * TPH, (n + 1) * TPH)
                        act.wait_ge(var_ready, var_c.next())
                        nc.scalar.activation(ln[:, 1, half], ln[:, 0, half], ACT.Sqrt).then_inc(std_ready, 1)

                    def normalize(t):
                        if t % TPH == 0:
                            act.wait_ge(ln_ready, ln_c.next())
                        nc.scalar.activation(h_sb[:, t % 4, :], src[:, t, :], ACT.Identity,
                                             scale=ln[:, 4, t:t + 1], bias=ln[:, 5, t:t + 1]).then_inc(h_ready, 1)

                    first = full_c.n

                    def hi(t):
                        unit = first + t + (router and t >= TPH)
                        act.wait_ge(aux_full, full_c.base + (unit + 1))
                        nc.scalar.activation(hT_hi[:, :, t * P:(t + 1) * P],
                                             queue_bank(unit).rearrange("p (c q) -> p c q", c=KC), ACT.Copy).then_inc(hi_ready, 1)

                    load_table(ACT.Sqrt)
                    std(0)
                    if after_std:
                        after_std()
                    for t in range(TPH):
                        normalize(t)
                    for t in range(TPH):
                        hi(t)
                    std(1)
                    for t in range(TPH, TT):
                        normalize(t)
                    for t in range(TPH, TT):
                        hi(t)

                def split_gu(s, j):
                    act.wait_ge(gu_in[s], gin_c[s].next() * 16)
                    nc.scalar.activation(sel[:, s, :], sel_all[:, bass.ds(j, 1), :], ACT.Copy)
                    nc.scalar.activation(gu_hi[:, s, :], gu_raw[:, s, :], ACT.Copy).then_inc(gu_hi_done, 1)

                def split_dn(s0):
                    act.wait_ge(dn_in, din_c.next() * 16)
                    nc.scalar.activation(dn_hi[:, s0:s0 + 2, :], dn_raw[:], ACT.Copy).then_inc(dn_hi_done, 1)

                def pair(p, split_next, first=False, s0=None):
                    s0 = s0 if s0 is not None else 2 * (p % 2)
                    if not first:
                        act.wait_ge(dn_full, dn_c.now())
                    if not (first and s0 == 0):
                        split_dn(s0)
                    for s in range(2):
                        for n in range(HALVES):
                            act.wait_ge(gate_full, gate_c.next())
                            act.wait_ge(acts_done, freed_c.next())
                            nc.scalar.activation(silu[:, n, :], gu_ps[:, n, :], ACT.Silu).then_inc(silu_ready, 1)
                        up_c.next(HALVES)
                        if split_next:
                            act.wait_ge(up_full, up_c.now())
                            if first and s0 == 0:
                                act.wait_ge(acts_done, up_c.now() + 2)
                            split_gu(s, p * 2 + 2 + s)

                def split_qk(g):
                    act.wait_ge(qk_w_in, qin_c.next() * 16)
                    nc.scalar.activation(qk_hi[:], qk_raw[:], ACT.Copy).then_inc(qk_w_hi, 1)


                def moe(src, first):
                    act.wait_ge(sel_in, seq * 16 + (16 if first else 32))
                    if first:
                        layer_norm(src, router=True, after_std=lambda: split_gu(0, 0))
                        split_gu(1, 1)
                    else:
                        split_gu(0, 0)
                        split_gu(1, 1)
                        layer_norm(src, router=True)
                    split_dn(0)
                    load_table(ACT.Exp)
                    act.wait_ge(shifted_ready, shifted_c.next())
                    nc.scalar.activation(expd[:], shifted[:], ACT.Exp).then_inc(exp_ready, 1)
                    pair(0, True, first=True)
                    pair(1, True, first=True)
                    per = {gin_c[0]: 2, gin_c[1]: 2, din_c: 2, gate_c: 4 * HALVES, up_c: 4 * HALVES,
                           freed_c: 4 * HALVES, dn_c: 2 * TT}
                    with act.Fori(0, LOOP_PAIRS) as i:
                        with looped(i, LOOP_PAIRS, per):
                            for k in range(2):
                                dn_c.next(TT)
                                pair(i * 2 + 2 + k, True, s0=2 * k)
                    dn_c.next(TT)
                    pair(PAIRS - 1, False)
                    act.wait_ge(up_full, up_c.now())
                    if first:
                        act.wait_ge(attn_w_in, seq * 32 + 16)
                        nc.scalar.activation(gu_hi[:], gu_raw[:], ACT.Copy).then_inc(attn_w_hi, 1)
                        split_qk(0)
                    dn_c.next(2 * TT)

                moe(x_first, True)
                full_c.n = MOE_AUX
                layer_norm(x_sb)
                drained_c.next(MOE_AUX + TT)

                def ones_for_max(slot):
                    for h in range(HG):
                        nc.scalar.activation(kst[slot][STACK:STACK + 2 * TT, h, :].rearrange("r (j k) -> r j k", k=P),
                                             key_rows[STACK:STACK + 2 * TT, :].unsqueeze(2).to_broadcast([2 * TT, TT, P]),
                                             ACT.Copy).then_inc(ones_in_stack, 1)

                def blocks_beta(h):
                    act.wait_ge(below_ready, below_c.next())
                    nc.scalar.activation(beta[:, :, h, 0:TT], below_max[:], ACT.Exp, scale=SCALE).then_inc(beta_ready, 1)

                def copy_block(step):
                    half, j = divmod(step, TT)
                    act.wait_ge(out_full, out_c.next())
                    if half:
                        act.wait_ge(aux_drained, drained_c.base + (drained_c.n + NUMBER[("block", half - 1, j)] + 1))
                    nc.scalar.activation(block_out[:, j, :], dn_ps[:, 0, :], ACT.Copy).then_inc(out_copied, 1)

                def v_tile(t):
                    act.wait_ge(v_full, seq * TT + (t + 1))
                    nc.scalar.activation(v_sb[:, t, :], gu_ps[:, t % 2, :], ACT.Copy).then_inc(v_drained, 1)

                for t in range(V_FIRST):
                    v_tile(t)
                for u in first_units():
                    if u == ("v", V_AHEAD):
                        act.wait_ge(aux_drained, drained_c.now())
                        ones_for_max(0)
                        nc.scalar.activation(beta[:].rearrange("p t h d -> p (t h d)"), hT_hi[:].rearrange("p c t -> p (c t)")[:, 0:TT * P],
                                             ACT.Copy, scale=0.0).then_inc(beta_zero, 1)
                        act.wait_ge(beta_zero, seq + 1)
                    if u[0] == "v":
                        v_tile(u[1])
                    if u == ("v", TT - 1):
                        ones_for_max(1)
                    if u[0] == "proj":
                        slot_free(act, seq, *u[1:])
                        act.wait_ge(aux_full, full_c.base + (MOE_AUX + TT + NUMBER[u] + 1))
                        nc.scalar.activation(proj_slots(*u[1:])[0], queue_bank(MOE_AUX + TT + NUMBER[u]),
                                             ACT.Copy).then_inc(hi_ready, 1)
                    if u == ("v", V_AHEAD + 1):
                        split_qk(1)
                    if u[0] == "A" and u[2][0] == "row" and u[2][2] == 0:
                        blocks_beta(u[2][1])
                for step, places in enumerate(attention_steps()):
                    if step < STEPS:
                        for pr in range(2):
                            act.wait_ge(scores_full, scores_c.next())
                            if pr == 0:
                                act.wait_ge(probs_used, used_c.next())
                            nc.scalar.activation(probsT[:, step % 2, 2 * pr:2 * pr + 2, :],
                                                 score_banks(step, pr), ACT.Exp, scale=SCALE).then_inc(probs_ready, 1)
                            if step and pr == (step % TT == 1):
                                copy_block(step - 1)
                    else:
                        copy_block(step - 1)
                    for u in sum(places, []):
                        if u[0] == "row" and u[2] == 0:
                            blocks_beta(u[1])
                    g = step // (HALVES * TT)
                    if step == g * HALVES * TT + SPLIT_STEP and g + 2 < GROUPS:
                        split_qk(g + 2)
                    if step == WO_STEP:
                        act.wait_ge(attn_w_in, seq * 32 + 32)
                        for halves in stack_in:
                            act.wait_ge(halves, (seq + 1) * (STACKED * UNIT_DMAS))
                        for head in head_in:
                            act.wait_ge(head, (seq + 1) * (GROUPS * HEAD_DMAS))
                        nc.scalar.activation(wo_hi[:], wo_raw[:], ACT.Copy).then_inc(attn_w_hi, 1)
                dn_c.next(TT)
                full_c.n = AUX - MOE_AUX
                moe(x_sb, False)
                assert dn_c.n == DN and gate_c.n == GU and used_c.n == STEPS

        @block.vector
        def _(dve):
            v = nc.vector
            dve.sem_inc(aux_drained, 2)
            dve.sem_inc(acts_done, 2)
            dve.sem_inc(gu_lo_done, 2)
            dve.sem_inc(dn_lo_done, 1)
            dve.sem_inc(dn_drained, 2)
            dve.sem_inc(sums_drained, 1)
            dve.wait_ge(consts_done, 2)
            for j in range(TT):
                ins = v.tensor_copy(block_rows[:, j, :].rearrange("p (h d) -> p h d", d=DH),
                                    ident[:].rearrange("p (h d) -> p h d", d=DH)[:, :, j:j + 1].to_broadcast([P, HG, DH]))
            ins.then_inc(router_ready, 1)
            v.tensor_reduce(in_head[:], ident[:].rearrange("p (h d) -> p h d", d=DH), AX.X, ALU.add).then_inc(router_ready, 1)
            dve.wait_ge(router_ready, 2)
            v.tensor_copy(head_rows[:].rearrange("p (h d) -> p h d", d=DH),
                          in_head[:].to_broadcast([P, HG, DH])).then_inc(router_ready, 1)
            dve.wait_ge(const_in, 32)
            v.tensor_copy(router[:, :, 0:NE], router_raw[:]).then_inc(router_ready, 1)
            dve.wait_ge(router_ready, 4)
            v.tensor_tensor(router[:, :, NE:2 * NE], router_raw[:], router[:, :, 0:NE].bitcast(F32),
                            ALU.subtract).then_inc(router_ready, 1)
            with dve.Fori(0, SEQS) as seq:
                step_c = Count(seq, STEP_LINKS)
                full_c, drained_c = Count(seq, AUX), Count(seq, AUX, 2)
                std_c, exp_c = Count(seq, 3 * HALVES), Count(seq, 2)
                silu_c, up_c = Count(seq, GU, 2), Count(seq, GU)
                acts_c, act_hi_c = Count(seq, GU, 2), Count(seq, GU)
                ghi_c, dhi_c = Count(seq, 2 * TILES, 2), Count(seq, 2 * PAIRS, 1)
                dn_c = Count(seq, DN)
                qhi_c = Count(seq, GROUPS)
                hi_c = Count(seq, 3 * TT + 2 * 2 * HALVES)

                def link(ins):
                    ins.then_inc(dve_step, 1)
                    dve.wait_ge(dve_step, step_c.next())

                def aux_unit():
                    bank = queue_bank(full_c.n)
                    dve.wait_ge(aux_full, full_c.next())
                    drained_c.next()
                    return bank

                def variance(n):
                    ts = slice(n * TPH, (n + 1) * TPH)
                    v.tensor_tensor(moments[:, 0, ts], stats[:, ts, 1], stats[:, ts, 4], ALU.add)
                    v.tensor_tensor(moments[:, 1, ts], stats[:, ts, 1], stats[:, ts, 4], ALU.subtract)
                    link(v.tensor_tensor(moments[:, 2, ts], stats[:, ts, 2], stats[:, ts, 5], ALU.add))
                    v.tensor_scalar(moments[:, 3, ts], moments[:, 2, ts], 1.0 / D, EPS, ALU.mult, ALU.add)
                    link(v.scalar_tensor_tensor(out=moments[:, 4, ts], in0=moments[:, 1, ts], scalar=0.25,
                                                in1=moments[:, 1, ts], op0=ALU.mult, op1=ALU.mult))
                    v.tensor_tensor(ln[:, 0, ts], moments[:, 3, ts], moments[:, 4, ts], ALU.add).then_inc(var_ready, 1)

                def rstd(n):
                    ts = slice(n * TPH, (n + 1) * TPH)
                    dve.wait_ge(std_ready, std_c.next())
                    link(v.reciprocal(ln[:, 2, ts], ln[:, 1, ts]))
                    link(v.tensor_tensor(ln[:, 3, ts], ln[:, 2, ts], ln[:, 2, ts], ALU.mult))
                    link(v.scalar_tensor_tensor(out=ln[:, 3, ts], in0=ln[:, 3, ts], scalar=-0.5, in1=ln[:, 0, ts],
                                                op0=ALU.mult, op1=ALU.mult))
                    link(v.scalar_tensor_tensor(out=ln[:, 4, ts], in0=ln[:, 3, ts], scalar=1.5, in1=ln[:, 2, ts],
                                                op0=ALU.add, op1=ALU.mult))
                    v.scalar_tensor_tensor(out=ln[:, 5, ts], in0=moments[:, 0, ts], scalar=-0.5, in1=ln[:, 4, ts],
                                           op0=ALU.mult, op1=ALU.mult).then_inc(ln_ready, 1)

                def tile_stats(t, src):
                    ins = v.bn_stats(stats[:, t, :], src[:, t, :])
                    if (t + 1) % TPH == 0:
                        link(ins)
                        variance(t // TPH)
                    if t == TPH:
                        rstd(0)

                def tile_added(t):
                    if 0 < t < TT - 1:
                        dve.wait_ge(dn_drained, dn_c.now() + 1)
                        tile_stats(t - 1, x_sb)

                def layer_norm(before=None, router=False, stats_left=(TT - 2, TT - 1)):
                    if before:
                        before()
                    for n in range(HALVES):
                        for t in range(n * TPH, (n + 1) * TPH):
                            cols = slice(t * P, (t + 1) * P)
                            ps = aux_unit().rearrange("p (c q) -> p c q", c=KC)
                            dve.wait_ge(hi_ready, hi_c.next())
                            v.tensor_tensor(hT_lo[:, :, cols], ps, hT_hi[:, :, cols].bitcast(F32),
                                            ALU.subtract).then_inc(aux_drained, 1)
                        if n == 0:
                            if stats_left:
                                dve.wait_ge(dn_drained, dn_c.now() + 2)
                            for t in stats_left:
                                tile_stats(t, x_sb)
                            rstd(1)
                        if router:
                            v.tensor_copy(logitsT_sb[:, n * BANK:(n + 1) * BANK],
                                          aux_unit()[0:2 * NE, :]).then_inc(aux_drained, 1)

                def route():
                    ps = aux_unit()[:, 0:TT * 2 * NE].rearrange("p (t e) -> p t e", t=TT)
                    link(v.tensor_copy(logits_lo[:], ps[:, :, NE:2 * NE]))
                    v.tensor_tensor(logits[:], ps[:, :, 0:NE], logits_lo[:], ALU.add).then_inc(aux_drained, 1)
                    dve.wait_ge(aux_drained, drained_c.now())
                    link(v.tensor_reduce(top[:], logits[:], AX.X, ALU.max))
                    v.tensor_tensor(shifted[:], logits[:], top[:].to_broadcast([P, TT, NE]),
                                    ALU.subtract).then_inc(shifted_ready, 1)
                    for e in range(NE):
                        for cols, op in ((slice(0, e + 1), ALU.is_gt), (slice(e + 1, NE), ALU.is_ge)):
                            k = cols.stop - cols.start
                            if k:
                                ins = v.tensor_tensor(beats[:, e, :, cols], logits[:, :, e:e + 1].to_broadcast([P, TT, k]),
                                                      logits[:, :, cols], op)
                    link(ins)
                    link(v.tensor_reduce(rank[:], beats[:].rearrange("p a t e -> p t e a"), AX.X, ALU.add))
                    dve.wait_ge(exp_ready, exp_c.next())
                    link(v.scalar_tensor_tensor(out=picked[:], in0=rank[:], scalar=2.0, in1=expd[:],
                                                op0=ALU.is_lt, op1=ALU.mult))
                    link(v.tensor_reduce(total[:], picked[:], AX.X, ALU.add))
                    link(v.reciprocal(inv_total[:], total[:]))
                    link(v.tensor_tensor(combine[:], picked[:], inv_total[:].to_broadcast([P, TT, NE]), ALU.mult))
                    link(v.tensor_copy(combine_s[:, :, 0:NE], combine[:]))
                    v.tensor_tensor(combine_s[:, :, NE:2 * NE], combine[:], combine_s[:, :, 0:NE].bitcast(F32),
                                    ALU.subtract).then_inc(combine_ready, 1)
                    for n in range(HALVES):
                        ps = aux_unit()
                        v.tensor_copy(combineT[:, n * BANK:(n + 1) * BANK], ps[0:2 * NE, :]).then_inc(aux_drained, 1)

                def split_gu(s):
                    dve.wait_ge(gu_hi_done, ghi_c.next())
                    v.tensor_tensor(gu_lo[:, s, :], gu_raw[:, s, :], gu_hi[:, s, :].bitcast(F32),
                                    ALU.subtract).then_inc(gu_lo_done, 1)

                def split_dn(s0):
                    dve.wait_ge(dn_hi_done, dhi_c.next())
                    v.tensor_tensor(dn_lo[:, s0:s0 + 2, :], dn_raw[:], dn_hi[:, s0:s0 + 2, :].bitcast(F32),
                                    ALU.subtract).then_inc(dn_lo_done, 1)

                def split_acts(slot, n):
                    cols = slice(n * BANK, (n + 1) * BANK)
                    v.tensor_copy(act_hi[:, slot, cols], acts[:, n, :]).then_inc(act_hi_done, 1)
                    dve.wait_ge(act_hi_done, act_hi_c.next())
                    v.tensor_tensor(act_lo[:, slot, cols], acts[:, n, :],
                                    act_hi[:, slot, cols].bitcast(F32), ALU.subtract).then_inc(act_ready, 1)

                def evacuate(s0, split_next, dn=True, split_last=False):
                    if dn:
                        split_dn(s0)
                    for s in range(2):
                        for n in range(HALVES):
                            dve.wait_ge(silu_ready, silu_c.next())
                            ps = aux_unit()
                            v.tensor_tensor(scaled[:, n, :], silu[:, n, :], ps, ALU.mult).then_inc(aux_drained, 1)
                            dve.wait_ge(up_full, up_c.next())
                            dve.wait_ge(aux_drained, drained_c.now())
                            v.tensor_tensor(acts[:, n, :], scaled[:, n, :], gu_ps[:, 2 + n, :],
                                            ALU.mult).then_inc(acts_done, 1)
                            dve.wait_ge(acts_done, acts_c.next())
                            if split_last or (s, n) != (1, HALVES - 1):
                                split_acts(s0 + s, n)
                        if s < split_next:
                            split_gu(s)

                def add_down(src=x_sb, between={}, last=False):
                    for t in range(TT):
                        if t in between:
                            between[t]()
                        at = dn_c.n % 2
                        dve.wait_ge(dn_full, dn_c.next())
                        v.scalar_tensor_tensor(out=x_sb[:, t, :], in0=dn_ps[:, at, :], scalar=0.5, in1=src[:, t, :],
                                               op0=ALU.mult, op1=ALU.add).then_inc(dn_drained, 1)
                        if last:
                            tile_added(t)

                def split_qk():
                    dve.wait_ge(qk_w_hi, qhi_c.next())
                    v.tensor_tensor(qk_lo[:], qk_raw[:], qk_hi[:].bitcast(F32), ALU.subtract).then_inc(qk_w_lo, 1)

                def split_v():
                    dve.wait_ge(attn_w_hi, seq * 2 + 1)
                    v.tensor_tensor(gu_lo[:], gu_raw[:], gu_hi[:].bitcast(F32), ALU.subtract).then_inc(attn_w_lo, 1)

                def rest_of(s0):
                    return {2: lambda: split_acts(s0 + 1, HALVES - 1), TPH + 2: lambda: split_gu(1)}

                def moe(first):
                    if first:
                        layer_norm(before=lambda: split_gu(0), router=True, stats_left=())
                        split_gu(1)
                    else:
                        layer_norm(router=True)
                    split_dn(0)
                    route()
                    evacuate(0, 2, dn=False, split_last=True)
                    evacuate(2, 1)
                    if first:
                        dve.wait_ge(x_free, seq + 1)
                    add_down(x_first if first else x_sb, between=rest_of(2))
                    per = {full_c: 4 * HALVES, drained_c: 4 * HALVES, silu_c: 4 * HALVES, up_c: 4 * HALVES,
                           acts_c: 4 * HALVES, act_hi_c: 4 * HALVES, ghi_c: 4, dhi_c: 2, dn_c: 2 * TT}
                    with dve.Fori(0, LOOP_PAIRS) as i:
                        with looped(i, LOOP_PAIRS, per):
                            evacuate(0, 1)
                            add_down(between=rest_of(0))
                            evacuate(2, 1)
                            add_down(between=rest_of(2))
                    evacuate(0, 0)
                    add_down(between={2: lambda: split_acts(1, HALVES - 1), **({3: split_v, TT - 2: split_qk} if first else {})})
                    add_down(last=first)

                for t in range(TT):
                    if t % TPH == 0:
                        dve.wait_ge(x_in[t // TPH], seq * 16 + 16)
                    tile_stats(t, x_first)
                moe(True)

                layer_norm()

                before_units = drained_c.now()

                def proj_unit(g, part, n):
                    hi, lo = proj_slots(g, part, n)
                    slot_free(dve, seq, g, part, n)
                    ps = aux_unit()
                    if g < 2:
                        dve.wait_ge(hi_ready, hi_c.next())
                    else:
                        link(v.tensor_copy(hi, ps))
                    v.tensor_tensor(lo, ps, hi.bitcast(F32), ALU.subtract).then_inc(aux_drained, 1)

                def a_unit(g, u):
                    if u[0] == "scores":
                        _, h, qt, kh = u
                        ps = aux_unit().rearrange("p (j k) -> p j k", k=P)
                        v.tensor_reduce(block_max[:, qt, kh * TPH:(kh + 1) * TPH], ps, AX.X, ALU.max).then_inc(aux_drained, 1)
                        if (qt, kh) == (TT - 1, HALVES - 1):
                            dve.wait_ge(aux_drained, drained_c.now())
                            v.tensor_scalar(neg_max[:], block_max[:], -1.0, None, ALU.mult)
                            link(v.tensor_reduce(full_max[:], block_max[:], AX.X, ALU.max))
                            if g or h:
                                dve.wait_ge(beta_ready, seq * HEADS + (g * HG + h))
                            v.tensor_tensor(below_max[:], block_max[:], full_max[:].to_broadcast([P, TT, TT]),
                                            ALU.subtract).then_inc(below_ready, 1)
                            link(v.tensor_copy(neg_max_s[:, :, :, 0], neg_max[:]))
                            v.tensor_tensor(neg_max_s[:, :, :, 1], neg_max[:], neg_max_s[:, :, :, 0].bitcast(F32),
                                            ALU.subtract).then_inc(max_ready, 1)
                    else:
                        _, h, n = u
                        ps = aux_unit()
                        v.tensor_copy(qst[g % 2][STACK:STACK + 2 * TT, h, n * BANK:(n + 1) * BANK],
                                      ps[0:2 * TT, :]).then_inc(aux_drained, 1)

                def weights(half):
                    n = half % HALVES
                    dve.wait_ge(probs_used, seq * STEPS + (2 + (half + 1) * TT))
                    if half:
                        dve.wait_ge(terms_added, seq * (GROUPS * HALVES * (TT - 1)) + (half * (TT - 1) - 1))
                    v.tensor_tensor(term[:, 0, :], dn_ps[:, 1, :], betaT[:, n * BANK:(n + 1) * BANK],
                                    ALU.mult).then_inc(sums_drained, 1)
                    dve.wait_ge(sums_drained, seq * (GROUPS * HALVES) + (half + 2))
                    link(v.tensor_copy(w_hi[:], term[:, 0, :]))
                    v.tensor_tensor(w_lo[:], term[:, 0, :], w_hi[:].bitcast(F32), ALU.subtract).then_inc(w_ready, 1)

                def finish_unit(u):
                    if u[0] == "sum":
                        ps = aux_unit()
                        v.tensor_copy(inv_sum[:], ps).then_inc(aux_drained, 1)
                        return
                    _, half, j = u
                    ps = aux_unit()
                    if j >= 3:
                        dve.wait_ge(terms_added, seq * (GROUPS * HALVES * (TT - 1)) + (half * (TT - 1) + j - 2))
                    if j == 0 and half > HALVES:
                        dve.wait_ge(outT_ready, seq * (GROUPS * HALVES) + half)
                    dve.wait_ge(out_copied, seq * STEPS + (half * TT + j + 2))
                    out = term[:, j % 2, :] if j else acc[:]
                    v.tensor_tensor(out, block_out[:, j, :], ps, ALU.mult).then_inc(aux_drained, 1)

                def invert(half, at):
                    if 0 <= half < GROUPS * HALVES - 1:
                        for k, place in enumerate(INVERT_AT[half % HALVES]):
                            if place == at:
                                dve.wait_ge(aux_drained, before_units + (NUMBER[("sum", half)] + 1))
                                quarter = inv_sum[:, k * P:(k + 1) * P]
                                v.reciprocal(quarter, quarter).then_inc(inv_ready, 1)

                def split_out(src, half):
                    g, n = divmod(half, HALVES)
                    cols = slice(n * BANK, (n + 1) * BANK)
                    link(v.tensor_copy(hT_hi[:, g, cols], src))
                    v.tensor_tensor(hT_lo[:, g, cols], src, hT_hi[:, g, cols].bitcast(F32),
                                    ALU.subtract).then_inc(outT_ready, 1)

                def finish(half):
                    if half < GROUPS * HALVES - 1:
                        dve.wait_ge(mean_ready, seq * (GROUPS * HALVES - 1) + (half + 1))
                    else:
                        link(v.reciprocal(inv_sum[:], inv_sum[:]))
                        dve.wait_ge(terms_added, seq * (GROUPS * HALVES * (TT - 1)) + (half + 1) * (TT - 1))
                        link(v.tensor_tensor(acc[:], acc[:], inv_sum[:], ALU.mult))
                    if half == HALVES:
                        for k in range(HALVES):
                            split_out(first_out[:, k, :], k)
                    if half >= HALVES:
                        split_out(acc[:], half)

                for u in first_units():
                    if u[0] == "proj":
                        proj_unit(*u[1:])
                    elif u == ("v", TT - 1):
                        split_qk()
                    elif u[0] == "A":
                        a_unit(0, u[2])
                for step, places in enumerate(attention_steps()):
                    g = step // (HALVES * TT)
                    if step == g * HALVES * TT + SPLIT_STEP + 1 and g + 2 < GROUPS:
                        split_qk()
                    if step == WO_STEP + 1:
                        dve.wait_ge(attn_w_hi, seq * 2 + 2)
                        v.tensor_tensor(wo_lo[:], wo_raw[:], wo_hi[:].bitcast(F32), ALU.subtract).then_inc(attn_w_lo, 1)
                    if step % TT == 1 and step > 2 * TT:
                        finish(step // TT - 2)
                    for place in range(3):
                        invert(step // TT - 1, (step % TT, place))
                        for u in places[place]:
                            if u[0] in ("scores", "row"):
                                a_unit(g + 1, u)
                            elif u[0] == "proj":
                                proj_unit(*u[1:])
                            elif u[0] == "beta":
                                v.tensor_copy(betaT[:, u[2] * BANK:(u[2] + 1) * BANK], aux_unit()).then_inc(aux_drained, 1)
                            else:
                                finish_unit(u)
                        if place == 1 and step and step % TT == 0:
                            weights(step // TT - 1)
                finish(GROUPS * HALVES - 2)
                for u in last_units():
                    finish_unit(u)
                split_gu(0)
                split_gu(1)
                dve.wait_ge(aux_drained, before_units + (NUMBER[("sum", GROUPS * HALVES - 1)] + 1))
                dve.wait_ge(bias_added, (seq + 1) * TT)
                for t in range(TT):
                    if t == 2:
                        finish(GROUPS * HALVES - 1)
                    at = dn_c.n % 2
                    dve.wait_ge(dn_full, dn_c.next())
                    v.tensor_tensor(x_sb[:, t, :], dn_ps[:, at, :], x_sb[:, t, :], ALU.add).then_inc(dn_drained, 1)
                    tile_added(t)
                moe(False)
                assert step_c.n == STEP_LINKS, step_c.n
                assert full_c.n == AUX and dn_c.n == DN and up_c.n == GU

        @block.tensor
        def _(pe):
            def product(ps, lhs, rhs, last=None):
                parts = [(c, a, b) for a, b in ((0, 0), (0, 1), (1, 0)) for c in range(KC)]
                for n, (c, a, b) in enumerate(parts):
                    mm = pe.matmul(ps, lhs(c, a), rhs(c, b), start=n == 0, stop=n == len(parts) - 1)
                return mm

            pe.sem_inc(probs_used, 2)
            pe.wait_ge(consts_done, 2)
            pe.wait_ge(router_ready, 5)
            with pe.Fori(0, SEQS) as seq:
                h_c = Count(seq, 3 * TT)
                aux_c = Count(seq, AUX)
                gate_c, up_c = Count(seq, GU), Count(seq, GU)
                ghi_c, glo_c = Count(seq, 2 * TILES, 2), Count(seq, 2 * TILES, 2)
                dhi_c, dlo_c = Count(seq, 2 * PAIRS, 1), Count(seq, 2 * PAIRS, 1)
                act_c = Count(seq, GU)
                dn_c = Count(seq, DN)
                cw_c = Count(seq, 2)
                qhi_c, qlo_c = Count(seq, GROUPS), Count(seq, GROUPS)
                max_c = Count(seq, HEADS)
                probs_c, scores_c = Count(seq, ST, 1), Count(seq, ST)

                def aux_bank():
                    k = aux_c.n
                    aux_c.next()
                    more = 2 if wide_queue(k) else after_norm_start(k) - 1 if after_norm_start(k) in (2, 3) else 0
                    pe.wait_ge(aux_drained, aux_c.ago(more) if more else aux_c.now())
                    return queue_bank(k)

                def drained(unit):
                    pe.wait_ge(aux_drained, aux_c.base + (unit + 1 + 2))

                def hT(lo, c, cols):
                    return (hT_lo if lo else hT_hi)[:, c, cols]

                def transposes(tiles):
                    for t in tiles:
                        pe.wait_ge(h_ready, h_c.next())
                        ps = aux_bank()
                        for c in range(KC):
                            mm = pe.transpose(ps[:, c * P:(c + 1) * P], h_sb[:, t % 4, c * P:(c + 1) * P], ident[:])
                        mm.then_inc(aux_full, 1)

                def weights(s, part):
                    return lambda c, lo: (gu_lo if lo else gu_hi)[:, s % 2, (part * KC + c) * P:(part * KC + c + 1) * P]

                def weights_split():
                    pe.wait_ge(gu_hi_done, ghi_c.next())
                    pe.wait_ge(gu_lo_done, glo_c.next())

                def gate(s, n):
                    pe.wait_ge(silu_ready, gate_c.next())
                    product(gu_ps[:, n, :], weights(s, 0),
                            lambda c, lo: hT(lo, c, slice(n * BANK, (n + 1) * BANK))).then_inc(gate_full, 1)

                def combine_weights(s, n):
                    ps = aux_bank()
                    pe.matmul(ps, sel[:, s % 2, :], combineT[:, n * BANK:(n + 1) * BANK],
                              start=True, stop=True).then_inc(aux_full, 1)

                def up(s, n):
                    pe.wait_ge(acts_done, up_c.next())
                    product(gu_ps[:, 2 + n, :], weights(s, 1),
                            lambda c, lo: hT(lo, c, slice(n * BANK, (n + 1) * BANK))).then_inc(up_full, 1)

                def gate_up():
                    for s in range(2):
                        weights_split()
                        for n in range(HALVES):
                            gate(s, n)
                            combine_weights(s, n)
                            up(s, n)

                def down(s0):
                    pe.wait_ge(act_ready, act_c.next(2 * HALVES))
                    pe.wait_ge(dn_hi_done, dhi_c.next())
                    pe.wait_ge(dn_lo_done, dlo_c.next())
                    for t in range(TT):
                        cols = slice(t * P, (t + 1) * P)
                        at = dn_c.n % 2
                        pe.wait_ge(dn_drained, dn_c.next())
                        parts = [(s, a, b) for a, b in ((0, 0), (0, 1), (1, 0)) for s in (s0, s0 + 1)]
                        for n, (s, a, b) in enumerate(parts):
                            mm = pe.matmul(dn_ps[:, at, :], (act_lo if a else act_hi)[:, s, cols],
                                           (dn_lo if b else dn_hi)[:, s, :], start=n == 0, stop=n == len(parts) - 1)
                        mm.then_inc(dn_full, 1)

                def logitsT(n):
                    cols = slice(n * BANK, (n + 1) * BANK)
                    ps = aux_bank()
                    for c in range(KC):
                        pe.matmul(ps[0:2 * NE, :], router[:, c, :], hT_hi[:, c, cols], start=c == 0, stop=False)
                    for c in range(KC):
                        mm = pe.matmul(ps[0:NE, :], router[:, c, 0:NE], hT_lo[:, c, cols], start=False, stop=c == KC - 1)
                    mm.then_inc(aux_full, 1)

                def logits():
                    drained(aux_c.n - 1)
                    ps = aux_bank()
                    for t in range(TT):
                        mm = pe.matmul(ps[:, t * 2 * NE:(t + 1) * 2 * NE], logitsT_sb[:, t * P:(t + 1) * P],
                                       ident[0:2 * NE, 0:2 * NE], start=True, stop=True)
                    mm.then_inc(aux_full, 1)

                def norm_banks():
                    pe.wait_ge(acts_done, up_c.now() + 2)

                def first_pair():
                    norm_banks()
                    transposes(range(TPH))
                    weights_split()
                    drained(aux_c.n - 1)
                    gate(0, 0)
                    logitsT(0)
                    transposes(range(TPH, TT))
                    drained(aux_c.n - 1)
                    logitsT(1)
                    up(0, 0)
                    logits()
                    gate(0, 1)
                    up(0, 1)
                    weights_split()
                    for n in range(HALVES):
                        gate(1, n)
                    combine_rows()
                    for n in range(HALVES):
                        combine_weights(0, n)
                    for n in range(HALVES):
                        combine_weights(1, n)
                        up(1, n)

                def moe():
                    first_pair()
                    gate_up()
                    down(0)
                    per = {aux_c: 4 * HALVES, gate_c: 4 * HALVES, up_c: 4 * HALVES, ghi_c: 4, glo_c: 4,
                           dhi_c: 2, dlo_c: 2, act_c: 4 * HALVES, dn_c: 2 * TT}
                    with pe.Fori(0, LOOP_PAIRS) as i:
                        with looped(i, LOOP_PAIRS, per):
                            gate_up()
                            down(2)
                            gate_up()
                            down(0)
                    gate_up()
                    down(2)
                    down(0)

                def combine_rows():
                    pe.wait_ge(combine_ready, cw_c.next())
                    for n in range(HALVES):
                        ps = aux_bank()
                        for q in range(TPH):
                            mm = pe.transpose(ps[0:2 * NE, q * P:(q + 1) * P],
                                              combine_s[:, n * TPH + q, :].bitcast(F32), ident[:])
                        mm.then_inc(aux_full, 1)
                    drained(aux_c.n - 1)

                moe()

                norm_banks()
                transposes(range(TPH))
                drained(aux_c.n - 1)
                pe.wait_ge(attn_w_hi, seq * 2 + 1)
                pe.wait_ge(attn_w_lo, seq * 2 + 1)

                def w512(c, lo):
                    w = (gu_lo if lo else gu_hi)[:].rearrange("p a (b d) -> p (a b) d", d=D)
                    return w[:, c, :]

                pe.wait_ge(silu_ready, gate_c.now() + 2)

                def v_tile(t):
                    pe.wait_ge(v_drained, seq * TT + (t + 1))
                    product(gu_ps[:, t % 2, :], lambda c, lo: hT(lo, c, slice(t * P, (t + 1) * P)), w512).then_inc(v_full, 1)

                for t in range(V_FIRST):
                    v_tile(t)
                transposes(range(TPH, TT))
                drained(aux_c.n - 1)

                def proj_unit(g, part, n):
                    if (part, n) == PROJ[0]:
                        pe.wait_ge(qk_w_hi, qhi_c.next())
                        pe.wait_ge(qk_w_lo, qlo_c.next())
                    ps = aux_bank()
                    product(ps, lambda c, lo: (qk_lo if lo else qk_hi)[:, part, c, :],
                            lambda c, lo: hT(lo, c, slice(n * BANK, (n + 1) * BANK))).then_inc(aux_full, 1)

                def a_unit(g, u):
                    if u[0] == "scores":
                        _, h, qt, kh = u
                        if qt == kh == 0:
                            pe.wait_ge(head_in[h], seq * (GROUPS * HEAD_DMAS) + (g + 1) * HEAD_DMAS)
                            for halves in stack_in if g and h == 0 else []:
                                pe.wait_ge(halves, seq * (STACKED * UNIT_DMAS) + g * UNIT_DMAS)
                        ps = aux_bank()
                        mm = pe.matmul(ps, qst[g % 2][0:STACK, h, qt * P:(qt + 1) * P],
                                       kst[g % 2][0:STACK, h, kh * BANK:(kh + 1) * BANK], start=True, stop=True)
                    else:
                        _, h, n = u
                        if n == 0:
                            pe.wait_ge(max_ready, max_c.next())
                        ps = aux_bank()
                        for c in range(TPH):
                            mm = pe.transpose(ps[0:2 * TT, c * P:(c + 1) * P],
                                              neg_max_s[:, n * TPH + c, :, :].rearrange("p j b -> p (j b)").bitcast(F32), ident[:])
                    mm.then_inc(aux_full, 1)

                def beta_unit(g, n):
                    if n == 0:
                        pe.wait_ge(beta_ready, seq * HEADS + (g + 1) * HG)
                    ps = aux_bank()
                    for c in range(TPH):
                        mm = pe.transpose(ps[:, c * P:(c + 1) * P],
                                          beta[:, n * TPH + c, :, :].rearrange("p h d -> p (h d)"), ident[:])
                    mm.then_inc(aux_full, 1)

                def finish_unit(u):
                    if u[0] == "block" and u[2] == 0:
                        pe.wait_ge(w_ready, seq * (GROUPS * HALVES) + (u[1] + 1))
                    lhs = head_rows[:] if u[0] == "sum" else block_rows[:, u[2], :]
                    ps = aux_bank()
                    pe.matmul(ps, lhs, w_hi[:], start=True, stop=False)
                    pe.matmul(ps, lhs, w_lo[:], start=False, stop=True).then_inc(aux_full, 1)

                def probs_v(step):
                    half, kt = divmod(step, TT)
                    g = half // HALVES
                    probs_c.next(2)
                    pe.wait_ge(probs_ready, probs_c.now())
                    pe.wait_ge(out_copied, seq * STEPS + (step + 1))
                    for h in range(HG):
                        mm = pe.matmul(dn_ps[h * DH:(h + 1) * DH, 0, :], v_sb[:, kt, g * P + h * DH:g * P + (h + 1) * DH],
                                       probsT[:, step % 2, h, :], start=True, stop=True, tile_position=(0, h * DH))
                    mm.then_inc(out_full, 1)

                def roinv_sums(step):
                    half, kt = divmod(step, TT)
                    if kt == 0:
                        pe.wait_ge(sums_drained, seq * (GROUPS * HALVES) + (half + 1))
                    for h in range(HG):
                        mm = pe.matmul(dn_ps[h * DH:(h + 1) * DH, 1, :], one_col[:, DH - 1 - kt:2 * DH - 1 - kt],
                                       probsT[:, step % 2, h, :], start=kt == 0, stop=kt == TT - 1,
                                       tile_position=(0, h * DH))
                    mm.then_inc(probs_used, 1)

                before_units = aux_c.n
                for u in first_units():
                    if u[0] == "v":
                        v_tile(u[1])
                    elif u[0] == "proj":
                        proj_unit(*u[1:])
                    else:
                        a_unit(0, u[2])
                pe.wait_ge(v_drained, (seq + 1) * TT + 2)
                for step, places in enumerate(attention_steps()):
                    g, at = divmod(step, HALVES * TT)
                    n, kt = divmod(at, TT)
                    if at == 0 and g < GROUPS:
                        drained(before_units + NUMBER[("A", g, ("row", HG - 1, HALVES - 1))])
                        if g < 2:
                            pe.wait_ge(ones_in_stack, seq * 2 * HG + (g + 1) * HG)
                    for place in range(3):
                        if place < 2 and step < STEPS:
                            scores_c.next()
                            pe.wait_ge(probs_ready, scores_c.ago(1) if step > LAST_GROUP else scores_c.now())
                            if step == LAST_GROUP and place == 0:
                                drained(aux_c.n - 1)
                            for h in (2 * place, 2 * place + 1):
                                mm = pe.matmul(score_banks(step, place)[:, h % 2, :], kst[g % 2][0:STACK + 2 * TT, h, kt * P:(kt + 1) * P],
                                               qst[g % 2][0:STACK + 2 * TT, h, n * BANK:(n + 1) * BANK], start=True, stop=True)
                            mm.then_inc(scores_full, 1)
                        if place == 2 and step:
                            roinv_sums(step - 1)
                        for u in places[place]:
                            if u[0] in ("scores", "row"):
                                a_unit(g + 1, u)
                            elif u[0] == "proj":
                                proj_unit(*u[1:])
                            elif u[0] == "beta":
                                beta_unit(*u[1:])
                            else:
                                finish_unit(u)
                        if place == 0 and step:
                            probs_v(step - 1)
                for u in last_units():
                    finish_unit(u)
                pe.wait_ge(out_copied, (seq + 1) * STEPS + 1)
                pe.wait_ge(attn_w_hi, seq * 2 + 2)
                pe.wait_ge(attn_w_lo, seq * 2 + 2)
                for t in range(TT):
                    if t % TPH == 0:
                        pe.wait_ge(outT_ready, seq * (GROUPS * HALVES) + (GROUPS * HALVES - 1 + t // TPH))
                    at = dn_c.n % 2
                    pe.wait_ge(dn_drained, dn_c.next())
                    product(dn_ps[:, at, :], lambda c, lo: hT(lo, c, slice(t * P, (t + 1) * P)),
                            lambda c, lo: (wo_lo if lo else wo_hi)[:, c, :]).then_inc(dn_full, 1)
                drained(aux_c.n - 1)
                moe()
                assert aux_c.n == AUX and dn_c.n == DN and up_c.n == GU

    return nc


def kernel(L0_attn_x, L0_attn_w_qkv, L0_attn_w_out, L0_attn_b_out, L0_ffn_gate_up_proj, L0_ffn_down_proj,
           L0_ffn_router_w):
    import numpy as np
    import concourse.bacc as bacc
    from concourse.bass_utils import run_bass_kernel_spmd

    def own(a):
        return np.ascontiguousarray(a)

    shape = L0_attn_x.shape
    D = shape[-1]
    KC = D // P
    E, H2, _ = L0_ffn_gate_up_proj.shape
    H = H2 // 2
    TILES = E * H // P
    gu = np.asarray(L0_ffn_gate_up_proj).reshape(E, 2, H, D).transpose(1, 0, 2, 3).reshape(2, TILES, P, KC, P)
    gu = own(gu.transpose(1, 4, 0, 3, 2)).reshape(TILES, P, 2 * KC * P)
    dn = np.asarray(L0_ffn_down_proj).transpose(0, 2, 1).reshape(TILES // 2, 2, P, D)
    dn = own(dn.transpose(0, 2, 1, 3)).reshape(TILES // 2, P, 2 * D)
    router = own(np.asarray(L0_ffn_router_w).T.reshape(KC, P, E).transpose(1, 0, 2))
    qkv = np.asarray(L0_attn_w_qkv)
    qk = own(qkv[:2 * D].reshape(2, KC, P, KC, P).transpose(1, 4, 0, 3, 2)).reshape(KC, P, 2 * KC * P)
    wv = own(qkv[2 * D:].T.reshape(KC, P, D).transpose(1, 0, 2)).reshape(P, KC * D)
    wo = own(np.asarray(L0_attn_w_out).T.reshape(KC, P, D).transpose(1, 0, 2)).reshape(P, KC * D)
    rows = np.arange(E * H) // H
    key_blocks = np.repeat(np.eye(L0_attn_x.shape[1] // P, dtype=np.float32), 2, axis=0)
    expert_rows = np.tile(np.equal(np.arange(E)[:, None], rows[None, :]), (2, 1)).astype(np.float32)

    arrays = {
        "x": own(np.asarray(L0_attn_x)).reshape(-1, D), "w_gu": gu, "w_dn": dn, "w_router": router, "w_qk": qk,
        "w_v": wv, "w_out": wo, "b_out": own(L0_attn_b_out), "expert_rows": expert_rows,
        "key_blocks": key_blocks,
    }
    nc = bacc.Bacc("TRN2", target_bir_lowering=False, num_devices=1)
    args = [nc.dram_tensor(n, a.shape, F32, kind="ExternalInput").ap() for n, a in arrays.items()]
    out = nc.dram_tensor("out", arrays["x"].shape, F32, kind="ExternalOutput").ap()
    macaron_block(nc, *args, out)
    result = run_bass_kernel_spmd(nc, [arrays], core_ids=[0])
    return result.results[0]["out"].reshape(shape)
```
